# Optimizing a Trainium2 kernel written in Bass

```python
import numpy as np
import jax
import jax.numpy as jnp

def _softmax(x, axis=-1):
    return jax.nn.softmax(x, axis=axis)

def _gelu(x):
    return jax.nn.gelu(x, approximate=True)

def _silu(x):
    return jax.nn.silu(x)

def _sigmoid(x):
    return jax.nn.sigmoid(x)

def _layernorm(x, axis=-1, eps=1e-05):
    m = jnp.mean(x, axis=axis, keepdims=True)
    v = jnp.var(x, axis=axis, keepdims=True)
    return (x - m) / jnp.sqrt(v + eps)

def _scatter_add(tgt, idx, src, axis=0):
    return tgt.at[idx].add(src)

def _segment_sum(src, seg, n):
    return jax.ops.segment_sum(src, seg, n)
kernel_name = 'mk_macaron_d1_jaxref_r8_69a2a2'

def setup_inputs(seed: int=0):
    np.random.seed(seed)
    _w = jnp.asarray

    def _L0_attn_setup():
        import jax, jax.numpy as jnp
        import numpy as np
        COSINE_SIM_SCALE = 8.0
        LN_EPS = 1e-05
        HEADS = 8

        def _l2norm(t, eps=1e-12):
            return t * jax.lax.rsqrt(jnp.sum(t * t, axis=-1, keepdims=True) + eps)
        key = jax.random.key(seed)
        k1, k2, k3 = jax.random.split(key, 3)
        b, n, dim = (2, 256, 128)
        inner = 64
        return {'x': jax.random.normal(k1, (b, n, dim), dtype=jnp.float32), 'ln_w': jnp.ones((dim,), dtype=jnp.float32), 'ln_b': jnp.zeros((dim,), dtype=jnp.float32), 'w_qkv': jax.random.normal(k2, (dim, 3 * inner), dtype=jnp.float32) * 0.02, 'w_out': jax.random.normal(k3, (inner, dim), dtype=jnp.float32) * 0.02}
    _L0_attn_in = _L0_attn_setup()

    def _L0_ffn_setup():
        import jax, jax.numpy as jnp
        import numpy as np
        TEMPERATURE = 0.5
        CAPACITY_FACTOR = 1.25
        TOP_K = 1
        key = jax.random.key(seed)
        ks = jax.random.split(key, 5)
        B, S, D, H, E = (4, 256, 128, 256, 8)
        s = 0.02
        return {'x': jax.random.normal(ks[0], (B, S, D), jnp.float32), 'gate_w': jax.random.normal(ks[1], (E, D), jnp.float32) * s, 'gate_b': jnp.zeros((E,), jnp.float32), 'rms_w': jnp.ones((E,), jnp.float32), 'w1': jax.random.normal(ks[2], (E, D, H), jnp.float32) * s, 'b1': jnp.zeros((E, H), jnp.float32), 'w2': jax.random.normal(ks[3], (E, H, D), jnp.float32) * s, 'b2': jnp.zeros((E, D), jnp.float32)}
    _L0_ffn_in = _L0_ffn_setup()
    _d = {'L0_attn_x': _L0_attn_in['x'], 'L0_attn_ln_w': _L0_attn_in['ln_w'], 'L0_attn_ln_b': _L0_attn_in['ln_b'], 'L0_attn_w_qkv': _L0_attn_in['w_qkv'], 'L0_attn_w_out': _L0_attn_in['w_out'], 'L0_ffn_gate_w': _L0_ffn_in['gate_w'], 'L0_ffn_gate_b': _L0_ffn_in['gate_b'], 'L0_ffn_rms_w': _L0_ffn_in['rms_w'], 'L0_ffn_w1': _L0_ffn_in['w1'], 'L0_ffn_b1': _L0_ffn_in['b1'], 'L0_ffn_w2': _L0_ffn_in['w2'], 'L0_ffn_b2': _L0_ffn_in['b2']}
    _x0 = _d['L0_attn_x']
    _d['L0_attn_x'] = jax.random.normal(jax.random.fold_in(jax.random.key(seed), 1), (2, 1024, 128), dtype=_x0.dtype)
    del _x0
    return _d

def reference(L0_attn_x, L0_attn_ln_w, L0_attn_ln_b, L0_attn_w_qkv, L0_attn_w_out, L0_ffn_gate_w, L0_ffn_gate_b, L0_ffn_rms_w, L0_ffn_w1, L0_ffn_b1, L0_ffn_w2, L0_ffn_b2):

    def _L0_attn_ref(x, ln_w, ln_b, w_qkv, w_out):
        import jax, jax.numpy as jnp
        import numpy as np
        COSINE_SIM_SCALE = 8.0
        LN_EPS = 1e-05
        HEADS = 8

        def _l2norm(t, eps=1e-12):
            return t * jax.lax.rsqrt(jnp.sum(t * t, axis=-1, keepdims=True) + eps)
        b, n, dim = x.shape
        h = HEADS
        mu = jnp.mean(x, axis=-1, keepdims=True)
        var = jnp.mean(jnp.square(x - mu), axis=-1, keepdims=True)
        xn = (x - mu) * jax.lax.rsqrt(var + LN_EPS) * ln_w + ln_b
        qkv = xn @ w_qkv
        q, k, v = jnp.split(qkv, 3, axis=-1)

        def to_heads(t):
            return t.reshape(b, n, h, -1).transpose(0, 2, 1, 3)
        q, k, v = map(to_heads, (q, k, v))
        q = _l2norm(q)
        k = _l2norm(k)
        sim = jnp.einsum('bhid,bhjd->bhij', q, k) * COSINE_SIM_SCALE
        causal_mask = jnp.tril(jnp.ones((n, n), dtype=bool))
        sim = jnp.where(causal_mask, sim, jnp.finfo(sim.dtype).min)
        attn = jax.nn.softmax(sim, axis=-1)
        o = jnp.einsum('bhij,bhjd->bhid', attn, v)
        o = o.transpose(0, 2, 1, 3).reshape(b, n, -1)
        return o @ w_out

    def _L0_ffn_ref(x, gate_w, gate_b, rms_w, w1, b1, w2, b2):
        import jax, jax.numpy as jnp
        import numpy as np
        TEMPERATURE = 0.5
        CAPACITY_FACTOR = 1.25
        TOP_K = 1
        B, S, D = x.shape
        E = gate_w.shape[0]
        xf = x.reshape(-1, D)
        N = xf.shape[0]
        logits = xf @ gate_w.T + gate_b
        eps = jnp.finfo(logits.dtype).eps
        ms = jnp.mean(logits * logits, axis=-1, keepdims=True)
        logits = logits * jax.lax.rsqrt(ms + eps) * rms_w
        gates = jax.nn.softmax(logits / TEMPERATURE, axis=-1)
        g, idx = jax.lax.top_k(gates, TOP_K)
        g, idx = (g[:, 0], idx[:, 0])
        capacity = min(int(np.ceil(N * TOP_K / E * CAPACITY_FACTOR)), N)
        counts = jnp.zeros((E,), jnp.int32).at[idx].add(1)
        active = (counts > 0) & (capacity >= 1)
        mask = active[idx].astype(gates.dtype)
        masked = g * mask
        norm_g = masked / (masked + 1e-06)
        h = jax.nn.gelu(jnp.einsum('nd,edh->neh', xf, w1) + b1, approximate=False)
        y = jnp.einsum('neh,ehd->ned', h, w2) + b2
        out = (y * norm_g[:, None, None]).sum(axis=1)
        return out.reshape(B, S, D)
    x = L0_attn_x
    x = x + 0.5 * _L0_ffn_ref(_layernorm(x, axis=-1), L0_ffn_gate_w, L0_ffn_gate_b, L0_ffn_rms_w, L0_ffn_w1, L0_ffn_b1, L0_ffn_w2, L0_ffn_b2)
    x = x + _L0_attn_ref(_layernorm(x, axis=-1), L0_attn_ln_w, L0_attn_ln_b, L0_attn_w_qkv, L0_attn_w_out)
    x = x + 0.5 * _L0_ffn_ref(_layernorm(x, axis=-1), L0_ffn_gate_w, L0_ffn_gate_b, L0_ffn_rms_w, L0_ffn_w1, L0_ffn_b1, L0_ffn_w2, L0_ffn_b2)
    return x

_drawn_inputs = setup_inputs


def setup_inputs(seed=0):
    import zlib

    import numpy as np

    out = dict(_drawn_inputs(seed))
    spreads = {'L0_attn_ln_w': (1.0, 0.6),
     'L0_attn_ln_b': (0.0, 0.8),
     'L0_ffn_gate_b': (0.0, 0.8),
     'L0_ffn_rms_w': (1.0, 0.6),
     'L0_ffn_b1': (0.0, 0.1),
     'L0_ffn_b2': (0.0, 0.1)}
    factors = {'L0_attn_w_qkv': 4.813, 'L0_attn_w_out': 4.617, 'L0_ffn_gate_w': 8.0}
    for name, (base, spread) in spreads.items():
        noise = np.random.default_rng([zlib.crc32(name.encode()), seed]).standard_normal(out[name].shape)
        drawn = base * np.exp(spread * noise) if base else spread * noise
        out[name] = jnp.asarray(drawn.astype(out[name].dtype))
    for name, factor in factors.items():
        out[name] = (out[name] * factor).astype(out[name].dtype)
    return out
```

```python
from contextlib import ExitStack

import concourse.bass as bass
import numpy as np
from concourse import mybir
from concourse.alu_op_type import AluOpType as ALU

P = 128
BATCH, SEQ, DIM = 2, 1024, 128
TOKENS = BATCH * SEQ
TILES = TOKENS // P
GROUP_TILES = 4
GROUP = GROUP_TILES * P
GROUPS = TOKENS // GROUP
EXPERTS, HIDDEN = 8, 256
CHUNKS = EXPERTS * HIDDEN // P
LAG = 3
RING = 4
HEADS, HEAD_DIM = 8, 8
INNER = HEADS * HEAD_DIM
QUADS = 2
STACK = 3 * HEAD_DIM
ROW = 32
SCALE = 8.0
LN_EPS = 1e-5
L2_EPS = 1e-12
RMS_EPS = float(np.finfo(np.float32).eps)
S_SETS = 3
P_SLOTS = 4
PV_LAG = 2
Q_GROUPS = SEQ // GROUP

BANK_H, BANK_Y, BANK_LN, BANK_YT, BANK_GATE = 0, 4, 5, 6, 7
BANK_QKV, BANK_QT, BANK_KT = 0, 2, 3
BANK_O, BANK_OT = 6, 7

COL_B1, COL_LNW, COL_LNB, COL_GATE = 0, CHUNKS, CHUNKS + 1, CHUNKS + 2
SMALL = CHUNKS + 2 + EXPERTS
COL_B2 = SMALL


def score_items(q_group):
    full = [[(kt, 0, GROUP, 0)] for kt in range(GROUP_TILES * q_group)]
    d = GROUP_TILES * q_group
    diagonal = [[(d, 0, 512, 0)], [(d + 1, 128, 384, 0), (d + 3, 384, 128, 384)], [(d + 2, 256, 256, 0)]]
    return full + diagonal


def build(nc, x, ln_w, ln_b, w_qkv, w_out, gate_w, gate_b, rms_w, w1, b1, w2, b2, out):
    f32, f32r, f16 = mybir.dt.float32, mybir.dt.float32r, mybir.dt.float16
    ACT = mybir.ActivationFunctionType
    AX = mybir.AxisListType
    ds = bass.ds

    x_d = x.rearrange("b (t p) d -> p (b t) d", p=P)
    out_d = out.rearrange("b (t p) d -> p (b t) d", p=P)

    ctx = ExitStack()
    with ctx:
        def sb(name, shape, dt=f32):
            return ctx.enter_context(nc.sbuf_tensor(name, shape, dt))

        def sem(name):
            return ctx.enter_context(nc.semaphore(name))

        x_sb = sb("x_sb", [P, TILES, DIM])
        xT_hi = sb("xT_hi", [P, TOKENS], f32r)
        xT_lo = sb("xT_lo", [P, TOKENS], f32r)
        xf = sb("xf", [P, GROUP])
        w1_raw = sb("w1_raw", [P, CHUNKS * P])
        w1_hi = sb("w1_hi", [P, CHUNKS * P], f32r)
        w1_lo = sb("w1_lo", [P, CHUNKS * P], f32r)
        w2_raw = sb("w2_raw", [P, CHUNKS * P])
        w2_hi = sb("w2_hi", [P, CHUNKS * P], f32r)
        w2_lo = sb("w2_lo", [P, CHUNKS * P], f32r)
        h = sb("h", [P, RING, GROUP])
        h_hi = sb("h_hi", [P, RING, GROUP], f32r)
        h_lo = sb("h_lo", [P, RING, GROUP], f32r)
        yT = sb("yT", [P, GROUP])
        small = sb("small", [SMALL, P])
        b2_sb = sb("b2_sb", [EXPERTS, P])
        cols = sb("cols", [P, SMALL + 1])
        gate_b_row = sb("gate_b_row", [P, EXPERTS])
        rms_w_row = sb("rms_w_row", [P, EXPERTS])
        wqkv_sb = sb("wqkv_sb", [P, 3 * INNER])
        wout_sb = sb("wout_sb", [INNER, DIM])
        ident = sb("ident", [P, P])
        ident16 = sb("ident16", [P, P], f16)
        ones = sb("ones", [P, P])
        neg_half = sb("neg_half", [P, 1])
        exp_two = sb("exp_two", [P, 1])
        ln_eps = sb("ln_eps", [P, 1])
        l2_eps = sb("l2_eps", [P, 1])
        fence = sb("fence", [P, 1])

        bn_part = sb("bn_part", [P, GROUP_TILES, 6])
        mean_var = sb("mean_var", [P, GROUP_TILES, 2])
        var_eps = sb("var_eps", [P, GROUP_TILES])
        rstd1 = sb("rstd1", [P, GROUP_TILES])
        rstd = sb("rstd", [P, GROUP_TILES])
        xn = sb("xn", [P, GROUP_TILES, DIM])

        logits = sb("logits", [P, GROUP_TILES, EXPERTS])
        gate_tmp = sb("gate_tmp", [P, GROUP_TILES, EXPERTS])
        gate_ms = sb("gate_ms", [P, GROUP_TILES])
        gate_rms = sb("gate_rms", [P, GROUP_TILES])
        gate_max = sb("gate_max", [P, GROUP_TILES])
        gate_e = sb("gate_e", [P, GROUP_TILES, EXPERTS])
        gate_sum = sb("gate_sum", [P, GROUP_TILES])
        gate_half = sb("gate_half", [P, GROUP_TILES])

        sq = sb("sq", [P, GROUP_TILES, 2 * INNER])
        ss = sb("ss", [P, GROUP_TILES, 2 * HEADS])
        rnorm = sb("rnorm", [P, GROUP_TILES, 2 * HEADS])
        qkn = sb("qkn", [P, 2, GROUP_TILES * HEADS, HEAD_DIM])
        q_stack = sb("q_stack", [P, GROUP_TILES * HEADS, ROW], f16)
        k_stack = sb("k_stack", [P, GROUP_TILES * HEADS, ROW], f16)
        qT = sb("qT", [P, QUADS, TOKENS], f16)
        kT = sb("kT", [P, QUADS, TOKENS], f16)
        v_ones = sb("v_ones", [P, TILES, HEADS, ROW])
        probs = sb("probs", [P, P_SLOTS, 2, GROUP])
        oT = sb("oT", [P, GROUP])
        rden = sb("rden", [P, GROUP_TILES, 4])
        o_tok = sb("o_tok", [P, GROUP_TILES, INNER])
        o_feat = sb("o_feat", [INNER, GROUP])

        ps = ctx.enter_context(nc.psum_tensor("ps", [P, 8, GROUP], f32))

        x_in = [sem(f"x_in{g}") for g in range(GROUPS)]
        small_in, b2_in, rows_in, wqkv_in, wout_in = (sem(n) for n in ("small_in", "b2_in", "rows_in", "wqkv_in", "wout_in"))
        w1_in = [sem(f"w1_in{k}") for k in range(4)]
        w2_in = [sem(f"w2_in{k}") for k in range(4)]
        out_stored = sem("out_stored")
        const_self, const_ready = sem("const_self"), sem("const_ready")
        small_t, cols_ready = sem("small_t"), sem("cols_ready")
        w1_hi_ready, w1_ready = sem("w1_hi_ready"), sem("w1_ready")
        w2_hi_ready, w2_ready = sem("w2_hi_ready"), sem("w2_ready")
        bn_done, mv_done, pool_ln, rstd_done = sem("bn_done"), sem("mv_done"), sem("pool_ln"), sem("rstd_done")
        xn_done, ln_t, xf_done = sem("xn_done"), sem("ln_t"), sem("xf_done")
        hi_done, xT_ready = sem("hi_done"), sem("xT_ready")
        gate_mm, gate_d1, gate_self, gate_p1, gate_d2, gate_p2, gate_pself, gate_ready = (
            sem(n) for n in ("gate_mm", "gate_d1", "gate_self", "gate_p1", "gate_d2", "gate_p2", "gate_pself", "gate_ready"))
        up_done, gelu_done, h_hi_done, split_done, down_done = (
            sem(n) for n in ("up_done", "gelu_done", "h_hi_done", "split_done", "down_done"))
        y_evac, y_t, resid = sem("y_evac"), sem("y_t"), sem("resid")
        qkv_mm, sq_done, ss_done, pool_ss, rnorm_done, qkn_done, hi16_done, stack_done, stack_t, qT_done, kT_done = (
            sem(n) for n in ("qkv_mm", "sq_done", "ss_done", "pool_ss", "rnorm_done", "qkn_done", "hi16_done", "stack_done",
                             "stack_t", "qT_done", "kT_done"))
        scores_done, exp_done, mask_done, pv_done = (sem(n) for n in ("scores_done", "exp_done", "mask_done", "pv_done"))
        o_copied, o_t, rden_done, o_normed, f_t, f_copied, proj_done, x_added = (
            sem(n) for n in ("o_copied", "o_t", "rden_done", "o_normed", "f_t", "f_copied", "proj_done", "x_added"))

        units = [(b, qg, quad) for b in range(BATCH) for qg in range(Q_GROUPS) for quad in range(QUADS)]
        steps = []
        for u, (b, qg, quad) in enumerate(units):
            items = score_items(qg)
            for k, item in enumerate(items):
                for pair in range(2):
                    steps.append(dict(unit=u, b=b, qg=qg, quad=quad, pair=pair, item=item, first=(k == 0),
                                      last=(k == len(items) - 1), local=2 * k + pair,
                                      diagonal=any(kt >= GROUP_TILES * qg for kt, *_ in item)))
        masks_until, n_masks = [], 0
        for st in steps:
            n_masks += len(st["item"]) if st["diagonal"] else 0
            masks_until.append(n_masks)
        steps_until_unit = [max(i for i, st in enumerate(steps) if st["unit"] == u) + 1 for u in range(len(units))]

        def groups_loop(eng, count, body):
            with eng.Fori(0, count) as g:
                body(g)

        block = ctx.enter_context(nc.Block())

        @block.sync
        def _(sp):
            w1_v = w1.rearrange("e d h -> d e h")
            w2_v = w2.rearrange("e (c p) d -> p (e c) d", p=P)
            sp.dma_start(x_sb[:, 0:4, :], x_d[:, 0:4, :]).then_inc(x_in[0], 16)
            sp.dma_start(small[0:CHUNKS, :], b1.rearrange("e (c p) -> (e c) p", p=P)).then_inc(small_in, 16)
            sp.dma_start(small[CHUNKS:CHUNKS + 1, :], ln_w.unsqueeze(0)).then_inc(small_in, 16)
            sp.dma_start(small[CHUNKS + 1:CHUNKS + 2, :], ln_b.unsqueeze(0)).then_inc(small_in, 16)
            sp.dma_start(small[CHUNKS + 2:SMALL, :], gate_w).then_inc(small_in, 16)
            sp.dma_start(b2_sb[:, :], b2).then_inc(b2_in, 16)
            for k in range(4):
                sp.dma_start(w1_raw[:, 512 * k:512 * k + 512].rearrange("d (e h) -> d e h", e=2),
                             w1_v[:, 2 * k:2 * k + 2, :]).then_inc(w1_in[k], 16)
            for k in range(4):
                sp.dma_start(w2_raw[:, 512 * k:512 * k + 512].rearrange("p (c d) -> p c d", c=4),
                             w2_v[:, 4 * k:4 * k + 4, :]).then_inc(w2_in[k], 16)
            for g in range(1, GROUPS):
                sp.dma_start(x_sb[:, 4 * g:4 * g + 4, :], x_d[:, 4 * g:4 * g + 4, :]).then_inc(x_in[g], 16)
            sp.dma_start(gate_b_row[:, :], gate_b.partition_broadcast(P)).then_inc(rows_in, 16)
            sp.dma_start(rms_w_row[:, :], rms_w.partition_broadcast(P)).then_inc(rows_in, 16)
            sp.dma_start(wqkv_sb[:, :], w_qkv).then_inc(wqkv_in, 16)
            sp.dma_start(wout_sb[:, :], w_out).then_inc(wout_in, 16)
            for g in range(GROUPS):
                sp.wait_ge(resid, GROUP_TILES * (GROUPS + g + 1))
                sp.dma_start(out_d[:, 4 * g:4 * g + 4, :], x_sb[:, 4 * g:4 * g + 4, :]).then_inc(out_stored, 16)
            sp.wait_ge(out_stored, 16 * GROUPS)

        @block.tensor
        def _(pe):
            def ln_transpose(n):
                pe.wait_ge(xn_done, GROUP_TILES * n + GROUP_TILES)
                pe.wait_ge(xf_done, n)
                for i in range(GROUP_TILES):
                    m = pe.transpose(ps[:, BANK_LN, P * i:P * i + P], xn[:, i, :], ident[:, :])
                m.then_inc(ln_t, 1)

            def gate_product(n, G):
                pe.wait_ge(xf_done, n + 1)
                pe.wait_ge(gate_d1, G)
                for i in range(GROUP_TILES):
                    m = pe.matmul(ps[:, BANK_GATE, EXPERTS * i:EXPERTS * i + EXPERTS], xf[:, P * i:P * i + P],
                                  cols[:, COL_GATE:COL_GATE + EXPERTS], start=True, stop=True)
                m.then_inc(gate_mm, 1)

            def up(n, c, g):
                pe.wait_ge(gelu_done, n - RING + 1)
                bank = ps[:, BANK_H + c % RING, :]
                w = slice(P * c, P * c + P)
                cols_g = ds(g * GROUP, GROUP)
                pe.matmul(bank, w1_hi[:, w], xT_hi[:, cols_g], start=True, stop=False)
                pe.matmul(bank, w1_hi[:, w], xT_lo[:, cols_g], start=False, stop=False)
                pe.matmul(bank, w1_lo[:, w], xT_hi[:, cols_g], start=False, stop=True).then_inc(up_done, 1)

            def down(n, c):
                pe.wait_ge(split_done, n + 1)
                w = slice(P * c, P * c + P)
                y = ps[:, BANK_Y, :]
                pe.matmul(y, w2_hi[:, w], h_hi[:, c % RING, :], start=(c == 0), stop=False)
                pe.matmul(y, w2_hi[:, w], h_lo[:, c % RING, :], start=False, stop=False)
                pe.matmul(y, w2_lo[:, w], h_hi[:, c % RING, :], start=False, stop=(c == CHUNKS - 1)).then_inc(down_done, 1)

            def ffn_group(layer, ln_base, g, last):
                G = GROUPS * layer + g
                for c in range(CHUNKS):
                    if c == 0:
                        pe.wait_ge(y_evac, G)
                        if layer == 0:
                            pe.wait_ge(w2_ready, 4)
                    down(CHUNKS * G + c, c)
                    ahead = c + LAG
                    if ahead < CHUNKS:
                        up(CHUNKS * G + ahead, ahead, g)
                    elif not last:
                        if ahead == CHUNKS:
                            pe.wait_ge(xT_ready, G + 2)
                        up(CHUNKS * G + ahead, ahead - CHUNKS, g + 1)
                    if c == 8 and not last:
                        ln_transpose(ln_base + g + 1)
                    if c == 10 and not last:
                        gate_product(ln_base + g + 1, G + 1)
                pe.wait_ge(y_evac, G + 1)
                pe.wait_ge(resid, GROUP_TILES * G)
                for i in range(GROUP_TILES):
                    m = pe.transpose(ps[:, BANK_YT, P * i:P * i + P], yT[:, P * i:P * i + P], ident[:, :])
                m.then_inc(y_t, 1)

            def ffn(layer, ln_base):
                ln_transpose(ln_base)
                pe.wait_ge(xT_ready, GROUPS * layer + 1)
                for c in range(LAG):
                    n = CHUNKS * GROUPS * layer + c
                    if layer == 0:
                        pe.wait_ge(w1_ready, 1)
                        bank_first(c)
                    else:
                        up(n, c, 0)
                if layer == 0:
                    pe.wait_ge(w1_ready, 4)
                gate_product(ln_base, GROUPS * layer)
                groups_loop(nc.tensor, GROUPS - 1, lambda g: ffn_group(layer, ln_base, g, False))
                ffn_group(layer, ln_base, GROUPS - 1, True)

            def bank_first(c):
                bank = ps[:, BANK_H + c, :]
                w = slice(P * c, P * c + P)
                pe.matmul(bank, w1_hi[:, w], xT_hi[:, 0:GROUP], start=True, stop=False)
                pe.matmul(bank, w1_hi[:, w], xT_lo[:, 0:GROUP], start=False, stop=False)
                pe.matmul(bank, w1_lo[:, w], xT_hi[:, 0:GROUP], start=False, stop=True).then_inc(up_done, 1)

            def attention_operands(g):
                n = GROUPS + g
                ln_transpose(n)
                pe.wait_ge(xf_done, n + 1)
                pe.wait_ge(qkn_done, 4 * g)
                for i in range(GROUP_TILES):
                    m = pe.matmul(ps[:, BANK_QKV + i // 2, 192 * (i % 2):192 * (i % 2) + 192], xf[:, P * i:P * i + P],
                                  wqkv_sb[:, :], start=True, stop=True)
                m.then_inc(qkv_mm, 1)
                pe.wait_ge(stack_done, 2 * g + 2)
                pe.wait_ge(qT_done, g)
                pe.wait_ge(kT_done, g)
                for stack, bank in ((q_stack, BANK_QT), (k_stack, BANK_KT)):
                    dst = ps[:, bank, :].bitcast(f16)
                    for quad in range(QUADS):
                        for i in range(GROUP_TILES):
                            src = stack[:, HEADS * i + 4 * quad:HEADS * i + 4 * quad + 4, :].rearrange("p h r -> p (h r)")
                            m = pe.transpose(dst[:, GROUP * quad + P * i:GROUP * quad + P * i + P], src, ident16[:, :])
                m.then_inc(stack_t, 1)

            def scores(s):
                st = steps[s]
                if s >= S_SETS:
                    pe.wait_ge(exp_done, s - S_SETS + 1)
                for hd in range(2):
                    j = 2 * st["pair"] + hd
                    rows = slice(ROW * j, ROW * j + STACK)
                    bank = 2 * (s % S_SETS) + hd
                    for kt, q0, width, at in st["item"]:
                        k0 = SEQ * st["b"] + P * kt
                        qc = SEQ * st["b"] + GROUP * st["qg"] + q0
                        m = pe.matmul(ps[:, bank, at:at + width], kT[rows, st["quad"], k0:k0 + P],
                                      qT[rows, st["quad"], qc:qc + width], start=True, stop=True)
                m.then_inc(scores_done, 1)

            def pv(s):
                st = steps[s]
                if st["first"] and st["pair"] == 0 and st["unit"] > 0:
                    pe.wait_ge(o_copied, st["unit"])
                if st["diagonal"]:
                    pe.wait_ge(mask_done, masks_until[s])
                else:
                    pe.wait_ge(exp_done, s + 1)
                for hd in range(2):
                    j = 2 * st["pair"] + hd
                    for n, (kt, q0, width, at) in enumerate(st["item"]):
                        m = pe.matmul(ps[ROW * j:ROW * j + ROW, BANK_O, q0:q0 + width],
                                      v_ones[:, SEQ // P * st["b"] + kt, 4 * st["quad"] + j, :],
                                      probs[:, s % P_SLOTS, hd, at:at + width],
                                      start=st["first"], stop=(st["last"] and n == len(st["item"]) - 1))
                m.then_inc(pv_done, 1)

            def output_rows(u):
                pe.wait_ge(o_copied, u + 1)
                if u >= 2:
                    pe.wait_ge(x_added, u // 2)
                if u % 2:
                    pe.wait_ge(o_normed, u)
                for i in range(GROUP_TILES):
                    m = pe.transpose(ps[:, BANK_OT, P * i:P * i + P], oT[:, P * i:P * i + P], ident[:, :])
                m.then_inc(o_t, 1)

            def output_features(u):
                pe.wait_ge(o_normed, u + 1)
                for i in range(GROUP_TILES):
                    m = pe.transpose(ps[0:INNER, BANK_OT, P * i:P * i + P], o_tok[:, i, :], ident[:, :])
                m.then_inc(f_t, 1)

            def project(u):
                pe.wait_ge(f_copied, u // 2 + 1)
                for i in range(GROUP_TILES):
                    m = pe.matmul(ps[:, BANK_OT, P * i:P * i + P], o_feat[:, P * i:P * i + P], wout_sb[:, :],
                                  start=True, stop=True)
                m.then_inc(proj_done, 1)

            def finish_unit(u, local):
                if local == 3:
                    output_rows(u)
                if u % 2 and local == 4:
                    output_features(u)
                if u % 2 and local == 5:
                    project(u)

            pe.wait_ge(const_ready, 1)
            pe.wait_ge(small_in, 64)
            pe.transpose(ps[:, BANK_GATE, 0:SMALL], small[:, :], ident[0:SMALL, 0:SMALL])
            pe.wait_ge(b2_in, 16)
            pe.matmul(ps[:, BANK_GATE, COL_B2:COL_B2 + 1], b2_sb[:, :], ones[0:EXPERTS, 0:1],
                      start=True, stop=True).then_inc(small_t, 1)
            pe.wait_ge(cols_ready, 1)
            ffn(0, 0)
            pe.wait_ge(wqkv_in, 16)
            pe.wait_ge(wout_in, 16)
            pe.wait_ge(gelu_done, CHUNKS * GROUPS)
            groups_loop(nc.tensor, GROUPS, attention_operands)
            pe.wait_ge(qT_done, GROUPS)
            pe.wait_ge(kT_done, GROUPS)
            pe.wait_ge(resid, GROUP_TILES * GROUPS)
            pe.wait_ge(gate_d1, GROUPS)
            for s in range(len(steps) + PV_LAG):
                if s < len(steps):
                    scores(s)
                if s >= PV_LAG:
                    pv(s - PV_LAG)
                if s < len(steps) and steps[s]["unit"] > 0:
                    finish_unit(steps[s]["unit"] - 1, steps[s]["local"])
            for local in range(3, 6):
                finish_unit(len(units) - 1, local)
            ffn(1, 2 * GROUPS)

        @block.scalar
        def _(act):
            def copy_features(n, ffn_groups, attention_groups, affine):
                act.wait_ge(ln_t, n + 1)
                act.wait_ge(xT_ready, ffn_groups)
                act.wait_ge(gate_mm, ffn_groups)
                act.wait_ge(qkv_mm, attention_groups)
                if affine:
                    nc.scalar.activation(xf[:, :], ps[:, BANK_LN, :], ACT.Identity, bias=cols[:, COL_LNB:COL_LNB + 1],
                                         scale=cols[:, COL_LNW:COL_LNW + 1]).then_inc(xf_done, 1)
                else:
                    nc.scalar.activation(xf[:, :], ps[:, BANK_LN, :], ACT.Copy).then_inc(xf_done, 1)

            def ffn_features(layer, n, G, g):
                copy_features(n, G, GROUPS if layer else 0, False)
                act.wait_ge(xf_done, n + 1)
                nc.scalar.activation(xT_hi[:, ds(g * GROUP, GROUP)], xf[:, :], ACT.Copy).then_inc(hi_done, 1)

            def gelu(n, c):
                act.wait_ge(up_done, n + 1)
                slot = c % RING
                bias = cols[:, COL_B1 + c:COL_B1 + c + 1]
                if not (isinstance(n, int) and n < RING):
                    act.wait_ge(split_done, n - RING + 1)
                    act.wait_ge(down_done, n - RING + 1)
                first = nc.scalar.activation(h[:, slot, :], ps[:, BANK_H + slot, :], ACT.Gelu, bias=bias)
                if c % 2 == 0:
                    nc.scalar.activation(h_hi[:, slot, :], ps[:, BANK_H + slot, :], ACT.Gelu, bias=bias).then_inc(gelu_done, 1)
                else:
                    first.then_inc(gelu_done, 1)

            def evacuate_y(G):
                act.wait_ge(down_done, CHUNKS * G + CHUNKS)
                act.wait_ge(y_t, G)
                nc.scalar.activation(yT[:, :], ps[:, BANK_Y, :], ACT.Identity,
                                     bias=cols[:, COL_B2:COL_B2 + 1]).then_inc(y_evac, 1)

            def ffn_group(layer, ln_base, g, last):
                G = GROUPS * layer + g
                for c in range(CHUNKS):
                    ahead = c + LAG
                    if c == CHUNKS - 1:
                        evacuate_y(G)
                    if ahead < CHUNKS or not last:
                        gelu(CHUNKS * G + ahead, ahead % CHUNKS)
                    if c == 9 and not last:
                        ffn_features(layer, ln_base + g + 1, G + 1, g + 1)

            def ffn(layer, ln_base):
                ffn_features(layer, ln_base, GROUPS * layer, 0)
                if layer == 0:
                    for k in range(4):
                        part = slice(512 * k, 512 * k + 512)
                        act.wait_ge(w2_in[k], 16)
                        nc.scalar.activation(w2_hi[:, part], w2_raw[:, part], ACT.Copy).then_inc(w2_hi_ready, 1)
                for c in range(LAG):
                    gelu(CHUNKS * GROUPS * layer + c, c)
                groups_loop(nc.scalar, GROUPS - 1, lambda g: ffn_group(layer, ln_base, g, False))
                ffn_group(layer, ln_base, GROUPS - 1, True)

            def attention_operands(g):
                n = GROUPS + g
                copy_features(n, GROUPS, g, True)
                act.wait_ge(qkv_mm, g + 1)
                act.wait_ge(ss_done, g)
                for half in range(2):
                    qkv = ps[:, BANK_QKV + half, 0:384].rearrange("p (t c) -> p t c", t=2)
                    nc.scalar.activation(sq[:, 2 * half:2 * half + 2, :], qkv[:, :, 0:2 * INNER], ACT.Square)
                    last = nc.scalar.activation(v_ones[:, ds(4 * g + 2 * half, 2), :, 0:HEAD_DIM],
                                                qkv[:, :, 2 * INNER:3 * INNER].rearrange("p t (h d) -> p t h d", h=HEADS),
                                                ACT.Copy)
                last.then_inc(sq_done, 1)
                act.wait_ge(stack_t, g + 1)
                nc.scalar.activation(kT[:, :, ds(g * GROUP, GROUP)],
                                     ps[:, BANK_KT, :].bitcast(f16).rearrange("p (a q) -> p a q", a=QUADS),
                                     ACT.Copy).then_inc(kT_done, 1)

            for k in range(4):
                part = slice(512 * k, 512 * k + 512)
                act.wait_ge(w1_in[k], 16)
                nc.scalar.activation(w1_hi[:, part], w1_raw[:, part], ACT.Copy).then_inc(w1_hi_ready, 1)
            act.wait_ge(cols_ready, 1)
            ffn(0, 0)
            act.wait_ge(const_ready, 3)
            groups_loop(nc.scalar, GROUPS, attention_operands)
            for s, st in enumerate(steps):
                act.wait_ge(scores_done, s + 1)
                if s >= P_SLOTS:
                    act.wait_ge(pv_done, s - P_SLOTS + 1)
                width = sum(w for _, _, w, _ in st["item"])
                bank = 2 * (s % S_SETS)
                nc.scalar.activation(probs[:, s % P_SLOTS, :, 0:width], ps[:, bank:bank + 2, 0:width], ACT.Exp,
                                     scale=SCALE).then_inc(exp_done, 1)
            ffn(1, 2 * GROUPS)

        @block.vector
        def _(dve):
            def stats(g, i):
                dve.bn_stats(bn_part[:, i, :], x_sb[:, ds(4 * g + i, 1), :].rearrange("p a d -> p (a d)")).then_inc(bn_done, 1)

            def wait_stats(n):
                dve.wait_ge(bn_done, GROUP_TILES * n + GROUP_TILES)
                dve.wait_ge(rstd_done, n)

            def aggregate(n):
                for i in range(GROUP_TILES):
                    dve.bn_aggr(mean_var[:, i, :], bn_part[:, i, :]).then_inc(mv_done, 1)

            def normalise(n, g):
                dve.wait_ge(rstd_done, n + 1)
                dve.wait_ge(ln_t, n)
                for i in range(GROUP_TILES):
                    dve.tensor_scalar(xn[:, i, :], x_sb[:, ds(4 * g + i, 1), :].rearrange("p a d -> p (a d)"),
                                      mean_var[:, i, 0:1], rstd[:, i:i + 1], ALU.subtract, ALU.mult).then_inc(xn_done, 1)

            def low_features(n, G, g):
                dve.wait_ge(hi_done, G + 1)
                part = ds(g * GROUP, GROUP)
                dve.tensor_tensor(xT_lo[:, part], xf[:, :], xT_hi[:, part].bitcast(f32), ALU.subtract).then_inc(xT_ready, 1)

            def gate_logits(G):
                dve.wait_ge(gate_mm, G + 1)
                dve.tensor_tensor(logits[:, :, :], ps[:, BANK_GATE, 0:GROUP_TILES * EXPERTS].rearrange("p (t e) -> p t e", e=EXPERTS),
                                  gate_b_row[:, :].unsqueeze(1).to_broadcast([P, GROUP_TILES, EXPERTS]), ALU.add).then_inc(gate_d1, 1)
                dve.wait_ge(gate_d1, G + 1)
                dve.tensor_tensor(gate_tmp[:, :, :], logits[:, :, :], logits[:, :, :], ALU.mult).then_inc(gate_self, 1)
                dve.wait_ge(gate_self, 6 * G + 1)
                dve.tensor_reduce(gate_ms[:, :], gate_tmp[:, :, :], AX.X, ALU.add).then_inc(gate_self, 1)
                dve.wait_ge(gate_self, 6 * G + 2)
                dve.tensor_scalar(gate_ms[:, :], gate_ms[:, :], 1.0 / EXPERTS, RMS_EPS, ALU.mult, ALU.add).then_inc(gate_self, 1)

            def gate_shift(G):
                dve.wait_ge(gate_p1, G + 1)
                dve.tensor_tensor(gate_tmp[:, :, :], logits[:, :, :],
                                  gate_rms[:, :].unsqueeze(2).to_broadcast([P, GROUP_TILES, EXPERTS]), ALU.mult).then_inc(gate_self, 1)
                dve.wait_ge(gate_self, 6 * G + 4)
                dve.tensor_tensor(logits[:, :, :], gate_tmp[:, :, :],
                                  rms_w_row[:, :].unsqueeze(1).to_broadcast([P, GROUP_TILES, EXPERTS]), ALU.mult).then_inc(gate_self, 1)
                dve.wait_ge(gate_self, 6 * G + 5)
                dve.tensor_reduce(gate_max[:, :], logits[:, :, :], AX.X, ALU.max).then_inc(gate_self, 1)
                dve.wait_ge(gate_self, 6 * G + 6)
                dve.tensor_tensor(gate_tmp[:, :, :], logits[:, :, :],
                                  gate_max[:, :].unsqueeze(2).to_broadcast([P, GROUP_TILES, EXPERTS]), ALU.subtract).then_inc(gate_d2, 1)

            def gate_weight(G):
                dve.wait_ge(gate_p2, G + 1)
                dve.tensor_reduce(gate_sum[:, :], gate_e[:, :, :], AX.X, ALU.add).then_inc(gate_ready, 1)
                dve.wait_ge(gate_ready, 3 * G + 1)
                dve.tensor_scalar(gate_sum[:, :], gate_sum[:, :], 2e-6, 2.0, ALU.mult, ALU.add).then_inc(gate_ready, 1)
                dve.wait_ge(gate_ready, 3 * G + 2)
                dve.reciprocal(gate_half[:, :], gate_sum[:, :]).then_inc(gate_ready, 1)

            def split(G, c):
                n = CHUNKS * G + c
                slot = c % RING
                dve.wait_ge(gelu_done, n + 1)
                if not (isinstance(n, int) and n < RING):
                    dve.wait_ge(down_done, n - RING + 1)
                if c % 2:
                    dve.tensor_copy(h_hi[:, slot, :], h[:, slot, :]).then_inc(h_hi_done, 1)
                    dve.wait_ge(h_hi_done, CHUNKS // 2 * G + (c + 1) // 2)
                dve.tensor_tensor(h_lo[:, slot, :], h[:, slot, :], h_hi[:, slot, :].bitcast(f32),
                                  ALU.subtract).then_inc(split_done, 1)

            def residual(G, g):
                dve.wait_ge(y_t, G + 1)
                dve.wait_ge(gate_ready, 3 * G + 3)
                for i in range(GROUP_TILES):
                    xi = x_sb[:, ds(4 * g + i, 1), :].rearrange("p a d -> p (a d)")
                    dve.scalar_tensor_tensor(xi, ps[:, BANK_YT, P * i:P * i + P], gate_half[:, i:i + 1], xi,
                                             ALU.mult, ALU.add).then_inc(resid, 1)

            def ffn_group(layer, ln_base, g, last):
                G = GROUPS * layer + g
                n = ln_base + g + 1
                for c in range(CHUNKS):
                    ahead = c + LAG
                    if c == 4 and not last:
                        wait_stats(n)
                    if ahead < CHUNKS or not last:
                        split(G + ahead // CHUNKS, ahead % CHUNKS)
                    if last:
                        continue
                    if c < GROUP_TILES:
                        stats(g + 1, c)
                        continue
                    if c == 4:
                        aggregate(n)
                    if c == 6:
                        normalise(n, g + 1)
                    if c == 10:
                        low_features(n, G + 1, g + 1)
                    if c == 11:
                        gate_logits(G + 1)
                    if c == 13:
                        gate_shift(G + 1)
                residual(G, g)
                if not last:
                    gate_weight(G + 1)

            def ffn(layer, ln_base):
                G = GROUPS * layer
                for i in range(GROUP_TILES):
                    stats(0, i)
                wait_stats(ln_base)
                aggregate(ln_base)
                normalise(ln_base, 0)
                if layer == 0:
                    for k in range(4):
                        part = slice(512 * k, 512 * k + 512)
                        dve.wait_ge(w1_hi_ready, k + 1)
                        dve.tensor_tensor(w1_lo[:, part], w1_raw[:, part], w1_hi[:, part].bitcast(f32),
                                          ALU.subtract).then_inc(w1_ready, 1)
                low_features(ln_base, G, 0)
                if layer == 0:
                    dve.wait_ge(rows_in, 32)
                gate_logits(G)
                gate_shift(G)
                gate_weight(G)
                for c in range(LAG):
                    split(G, c)
                if layer == 0:
                    for g in range(1, GROUPS):
                        dve.wait_ge(x_in[g], 16)
                groups_loop(nc.vector, GROUPS - 1, lambda g: ffn_group(layer, ln_base, g, False))
                ffn_group(layer, ln_base, GROUPS - 1, True)

            def attention_operands(g):
                n = GROUPS + g
                for i in range(GROUP_TILES):
                    stats(g, i)
                wait_stats(n)
                dve.memset(fence[:, :], 0.0)
                aggregate(n)
                normalise(n, g)
                dve.wait_ge(sq_done, g + 1)
                dve.tensor_reduce(ss[:, :, :].rearrange("p t h -> p (t h)"),
                                  sq[:, :, :].rearrange("p t (h d) -> p (t h) d", d=HEAD_DIM), AX.X, ALU.add).then_inc(ss_done, 1)
                dve.wait_ge(rnorm_done, g + 1)
                for half in range(2):
                    qkv = ps[:, BANK_QKV + half, 0:384].rearrange("p (t c) -> p t c", t=2)
                    for which in range(2):
                        dve.tensor_tensor(
                            qkn[:, which, 16 * half:16 * half + 16, :].rearrange("p (t h) d -> p t h d", t=2),
                            qkv[:, :, INNER * which:INNER * which + INNER].rearrange("p t (h d) -> p t h d", h=HEADS),
                            rnorm[:, 2 * half:2 * half + 2, HEADS * which:HEADS * which + HEADS].unsqueeze(3)
                            .to_broadcast([P, 2, HEADS, HEAD_DIM]), ALU.mult).then_inc(qkn_done, 1)
                dve.wait_ge(qkn_done, 4 * g + 4)
                dve.wait_ge(stack_t, g)
                hi_q = q_stack[:, :, 0:2 * HEAD_DIM].rearrange("p h (a d) -> p h a d", a=2)
                hi_k = k_stack[:, :, 0:4 * HEAD_DIM].rearrange("p h (a b d) -> p h a b d", a=2, b=2)[:, :, :, 0, :]
                for dst, which in ((hi_q, 0), (hi_k, 1)):
                    dve.tensor_copy(dst, qkn[:, which, :, :].unsqueeze(2).to_broadcast([P, GROUP_TILES * HEADS, 2, HEAD_DIM])
                                    ).then_inc(hi16_done, 1)
                dve.wait_ge(hi16_done, 2 * g + 2)
                for stack, which, at in ((q_stack, 0, 2 * HEAD_DIM), (k_stack, 1, HEAD_DIM)):
                    dve.tensor_tensor(stack[:, :, at:at + HEAD_DIM], qkn[:, which, :, :], stack[:, :, 0:HEAD_DIM],
                                      ALU.subtract).then_inc(stack_done, 1)
                dve.wait_ge(stack_t, g + 1)
                dve.tensor_copy(qT[:, :, ds(g * GROUP, GROUP)],
                                ps[:, BANK_QT, :].bitcast(f16).rearrange("p (a q) -> p a q", a=QUADS)).then_inc(qT_done, 1)

            def finish_unit(u):
                b, qg, quad = units[u]
                dve.wait_ge(pv_done, steps_until_unit[u])
                dve.wait_ge(o_t, u)
                dve.tensor_copy(oT[:, :], ps[:, BANK_O, :]).then_inc(o_copied, 1)
                dve.wait_ge(o_t, u + 1)
                rows = ps[:, BANK_OT, :].rearrange("p (t h r) -> p t h r", t=GROUP_TILES, h=4)
                dve.reciprocal(rden[:, :, :], rows[:, :, :, HEAD_DIM]).then_inc(rden_done, 1)
                dve.wait_ge(rden_done, u + 1)
                dve.tensor_tensor(o_tok[:, :, 4 * HEAD_DIM * quad:4 * HEAD_DIM * (quad + 1)].rearrange("p t (h d) -> p t h d", h=4),
                                  rows[:, :, :, 0:HEAD_DIM],
                                  rden[:, :, :].unsqueeze(3).to_broadcast([P, GROUP_TILES, 4, HEAD_DIM]),
                                  ALU.mult).then_inc(o_normed, 1)
                if quad == QUADS - 1:
                    dve.wait_ge(f_t, u // 2 + 1)
                    dve.tensor_copy(o_feat[:, :], ps[0:INNER, BANK_OT, :]).then_inc(f_copied, 1)
                    dve.wait_ge(proj_done, u // 2 + 1)
                    t0 = SEQ // P * b + GROUP_TILES * qg
                    xi = x_sb[:, t0:t0 + GROUP_TILES, :].rearrange("p t d -> p (t d)")
                    dve.tensor_tensor(xi, ps[:, BANK_OT, :], xi, ALU.add).then_inc(x_added, 1)

            dve.wait_ge(small_t, 1)
            dve.tensor_copy(cols[:, :], ps[:, BANK_GATE, 0:SMALL + 1]).then_inc(cols_ready, 1)
            dve.wait_ge(x_in[0], 16)
            ffn(0, 0)
            dve.wait_ge(resid, GROUP_TILES * GROUPS)
            dve.wait_ge(const_ready, 3)
            groups_loop(nc.vector, GROUPS, attention_operands)
            for u in range(len(units)):
                finish_unit(u)
            dve.wait_ge(x_added, len(units) // 2)
            ffn(1, 2 * GROUPS)

        @block.gpsimd
        def _(pool):
            def rstd_plain(n):
                pool.wait_ge(mv_done, GROUP_TILES * n + GROUP_TILES)
                pool.tensor_tensor(var_eps[:, :], mean_var[:, :, 1], ln_eps[:, 0:1].to_broadcast([P, GROUP_TILES]), ALU.add).then_inc(pool_ln, 1)

            def power(dst, src):
                return pool.tensor_tensor(dst, src, neg_half[:, 0:1].to_broadcast([P, GROUP_TILES]), ALU.pow)

            def ln_once(n, k):
                rstd_plain(n)
                pool.wait_ge(pool_ln, k + 1)
                pool.wait_ge(xn_done, GROUP_TILES * n)
                power(rstd[:, :], var_eps[:, :]).then_inc(rstd_done, 1)

            def ln_twice(n, k):
                rstd_plain(n)
                pool.wait_ge(pool_ln, k + 1)
                power(rstd1[:, :], var_eps[:, :]).then_inc(pool_ln, 1)
                pool.wait_ge(pool_ln, k + 2)
                pool.tensor_tensor(var_eps[:, :], rstd1[:, :], rstd1[:, :], ALU.mult).then_inc(pool_ln, 1)
                pool.wait_ge(pool_ln, k + 3)
                pool.tensor_tensor(var_eps[:, :], var_eps[:, :], mean_var[:, :, 1], ALU.mult).then_inc(pool_ln, 1)
                pool.wait_ge(pool_ln, k + 4)
                pool.tensor_tensor(var_eps[:, :], var_eps[:, :], ln_eps[:, 0:1].to_broadcast([P, GROUP_TILES]), ALU.add).then_inc(pool_ln, 1)
                pool.wait_ge(pool_ln, k + 5)
                power(var_eps[:, :], var_eps[:, :]).then_inc(pool_ln, 1)
                pool.wait_ge(pool_ln, k + 6)
                pool.wait_ge(xn_done, GROUP_TILES * n)
                pool.tensor_tensor(rstd[:, :], var_eps[:, :], rstd1[:, :], ALU.mult).then_inc(rstd_done, 1)

            def gate(G):
                pool.wait_ge(gate_self, 6 * G + 3)
                power(gate_rms[:, :], gate_ms[:, :]).then_inc(gate_p1, 1)
                pool.wait_ge(gate_d2, G + 1)
                pool.tensor_tensor(gate_e[:, :, :], exp_two[:, 0:1].unsqueeze(2).to_broadcast([P, GROUP_TILES, EXPERTS]),
                                   gate_tmp[:, :, :], ALU.pow).then_inc(gate_p2, 1)

            def ffn(layer, ln_base, k):
                G = GROUPS * layer
                ln_once(ln_base, k)
                if layer == 0:
                    for part_k in range(4):
                        part = slice(512 * part_k, 512 * part_k + 512)
                        pool.wait_ge(w2_hi_ready, part_k + 1)
                        pool.tensor_tensor(w2_lo[:, part], w2_raw[:, part], w2_hi[:, part].bitcast(f32),
                                           ALU.subtract).then_inc(w2_ready, 1)
                gate(G)

                def body(g):
                    ln_once(ln_base + g + 1, k + g + 1)
                    gate(G + g + 1)
                groups_loop(nc.gpsimd, GROUPS - 1, body)

            def attention_operands(g):
                n = GROUPS + g
                ln_twice(n, GROUPS + 6 * g)
                pool.wait_ge(ss_done, g + 1)
                pool.wait_ge(qkn_done, 4 * g)
                flat = rnorm[:, :, :].rearrange("p t h -> p (t h)")
                pool.tensor_tensor(flat, ss[:, :, :].rearrange("p t h -> p (t h)"),
                                   l2_eps[:, 0:1].to_broadcast([P, GROUP_TILES * 2 * HEADS]), ALU.add).then_inc(pool_ss, 1)
                pool.wait_ge(pool_ss, g + 1)
                pool.tensor_tensor(flat, flat, neg_half[:, 0:1].to_broadcast([P, GROUP_TILES * 2 * HEADS]),
                                   ALU.pow).then_inc(rnorm_done, 1)

            pool.memset(neg_half[:, :], -0.5).then_inc(const_self, 1)
            pool.memset(exp_two[:, :], float(np.exp(2.0))).then_inc(const_self, 1)
            pool.memset(ln_eps[:, :], LN_EPS).then_inc(const_self, 1)
            pool.memset(l2_eps[:, :], L2_EPS).then_inc(const_self, 1)
            pool.memset(ones[:, :], 1.0).then_inc(const_self, 1)
            pool.wait_ge(const_self, 5)
            pool.affine_select(ident[:, :], ones[:, :], [[1, P]], ALU.is_equal, 0.0, base=0,
                               channel_multiplier=-1).then_inc(const_ready, 1)
            pool.wait_ge(const_ready, 1)
            pool.tensor_copy(ident16[:, :], ident[:, :]).then_inc(const_ready, 1)
            pool.memset(v_ones[:, :, :, :].rearrange("p t h r -> p (t h r)"), 0.0).then_inc(const_self, 1)
            pool.memset(q_stack[:, :, :].rearrange("p h r -> p (h r)"), 0.0).then_inc(const_self, 1)
            pool.memset(k_stack[:, :, :].rearrange("p h r -> p (h r)"), 0.0).then_inc(const_self, 1)
            pool.wait_ge(const_self, 8)
            pool.memset(v_ones[:, :, :, HEAD_DIM:HEAD_DIM + 1].rearrange("p t h r -> p (t h) r"), 1.0).then_inc(const_ready, 1)
            ffn(0, 0, 0)
            groups_loop(nc.gpsimd, GROUPS, attention_operands)
            for s, st in enumerate(steps):
                if not st["diagonal"]:
                    continue
                pool.wait_ge(exp_done, s + 1)
                for _, _, _, at in st["item"]:
                    region = probs[:, s % P_SLOTS, :, at:at + P]
                    pool.affine_select(region, region, [[0, 2], [1, P]], ALU.is_ge, 0.0, base=0,
                                       channel_multiplier=-1).then_inc(mask_done, 1)
            ffn(1, 2 * GROUPS, GROUPS + 6 * GROUPS)


_INPUTS = ["L0_attn_x", "L0_attn_ln_w", "L0_attn_ln_b", "L0_attn_w_qkv", "L0_attn_w_out", "L0_ffn_gate_w", "L0_ffn_gate_b",
           "L0_ffn_rms_w", "L0_ffn_w1", "L0_ffn_b1", "L0_ffn_w2", "L0_ffn_b2"]


def kernel(**inputs):
    import concourse.bacc as bacc
    from concourse.bass_utils import run_bass_kernel_spmd

    nc = bacc.Bacc("TRN2", target_bir_lowering=False, num_devices=1)
    arrays, args = {}, []
    for name in _INPUTS:
        a = np.ascontiguousarray(inputs[name])
        arrays[f"in_{name}"] = a
        args.append(nc.dram_tensor(f"in_{name}", a.shape, mybir.dt.from_np(a.dtype), kind="ExternalInput").ap())
    out = nc.dram_tensor("out_x", (BATCH, SEQ, DIM), mybir.dt.float32, kind="ExternalOutput").ap()
    build(nc, *args, out)
    return run_bass_kernel_spmd(nc, [arrays], core_ids=[0]).results[0]["out_x"]
```

```python
from contextlib import ExitStack

import concourse.bass as bass
import numpy as np
from concourse import mybir
from concourse.alu_op_type import AluOpType as ALU

P = 128
BATCH, SEQ, DIM = 2, 1024, 128
TOKENS = BATCH * SEQ
TILES = TOKENS // P
GROUP_TILES = 4
GROUP = GROUP_TILES * P
GROUPS = TOKENS // GROUP
EXPERTS, HIDDEN = 8, 256
CHUNKS = EXPERTS * HIDDEN // P
WARM_UP = 14
LAG = 3
RING = 4
HEADS, HEAD_DIM = 8, 8
INNER = HEADS * HEAD_DIM
QUADS = 2
STACK = 3 * HEAD_DIM
ROW = 32
SCALE = 8.0
LN_EPS = 1e-5
L2_EPS = 1e-12
RMS_EPS = float(np.finfo(np.float32).eps)
S_SETS = 3
P_SLOTS = 8
PV_LAG = 3
FFN, ATT = 0, 1
Q_GROUPS = SEQ // GROUP

BANK_H, BANK_Y, BANK_LN, BANK_YT, BANK_GATE = 0, 4, 5, 5, 7
BANK_YT_LAST = 6
BANK_QT, BANK_KT = 6, 7

COL_B1, COL_LNW, COL_LNB, COL_GATE = 0, CHUNKS, CHUNKS + 1, CHUNKS + 2
SMALL = CHUNKS + 2 + EXPERTS
COL_B2 = SMALL


def score_items(q_group):
    full = [[(kt, 0, GROUP, 0)] for kt in range(GROUP_TILES * q_group)]
    d = GROUP_TILES * q_group
    diagonal = [[(d, 0, 512, 0)], [(d + 1, 128, 384, 0), (d + 3, 384, 128, 384)], [(d + 2, 256, 256, 0)]]
    return full + diagonal


def build(nc, x, ln_w, ln_b, w_qkv, w_out, gate_w, gate_b, rms_w, w1, b1, w2, b2, out):
    f32, f32r, f16 = mybir.dt.float32, mybir.dt.float32r, mybir.dt.float16
    ACT = mybir.ActivationFunctionType
    AX = mybir.AxisListType
    ds = bass.ds

    x_d = x.rearrange("b (t p) d -> p (b t) d", p=P)
    out_d = out.rearrange("b (t p) d -> p (b t) d", p=P)

    ctx = ExitStack()
    with ctx:
        def sb(name, shape, dt=f32):
            return ctx.enter_context(nc.sbuf_tensor(name, shape, dt))

        def sem(name):
            return ctx.enter_context(nc.semaphore(name))

        x_sb = sb("x_sb", [P, TILES, DIM])
        xT_hi = sb("xT_hi", [P, TOKENS], f32r)
        xT_lo = sb("xT_lo", [P, TOKENS], f32r)
        xf = sb("xf", [P, 2, GROUP])
        w_raw = sb("w_raw", [P, 2 * CHUNKS * P])
        w1_raw, w2_raw = w_raw[:, 0:CHUNKS * P], w_raw[:, CHUNKS * P:2 * CHUNKS * P]
        w1_hi = sb("w1_hi", [P, CHUNKS * P], f32r)
        w1_lo = sb("w1_lo", [P, CHUNKS * P], f32r)
        w2_hi = sb("w2_hi", [P, CHUNKS * P], f32r)
        w2_lo = sb("w2_lo", [P, CHUNKS * P], f32r)
        h = sb("h", [P, RING, GROUP])
        h_hi = sb("h_hi", [P, RING, GROUP], f32r)
        h_lo = sb("h_lo", [P, RING, GROUP], f32r)
        yT = sb("yT", [P, GROUP])
        small = sb("small", [SMALL, P])
        b2_sb = sb("b2_sb", [EXPERTS, P])
        cols = sb("cols", [P, SMALL + 1])
        gate_b_row = sb("gate_b_row", [P, EXPERTS])
        rms_w_row = sb("rms_w_row", [P, EXPERTS])
        wqkv_sb = sb("wqkv_sb", [P, 3 * INNER])
        wout_sb = sb("wout_sb", [INNER, DIM])
        ident = sb("ident", [P, P])
        ident16 = sb("ident16", [P, P], f16)
        ones = sb("ones", [P, P])
        table_use = sb("table_use", [P, 2])
        neg_half = sb("neg_half", [P, 1])
        ln_eps = sb("ln_eps", [P, 1])

        bn_part = sb("bn_part", [P, 2, GROUP_TILES, 6])
        mean_var = sb("mean_var", [P, 2, GROUP_TILES, 2])
        var_eps = sb("var_eps", [P, 2, GROUP_TILES])
        rstd1 = sb("rstd1", [P, GROUP_TILES])
        rstd = sb("rstd", [P, 2, GROUP_TILES])
        xn = sb("xn", [P, 2, GROUP_TILES, DIM])

        logits = sb("logits", [P, GROUP_TILES, EXPERTS])
        gate_tmp = sb("gate_tmp", [P, GROUP_TILES, EXPERTS])
        gate_ms = sb("gate_ms", [P, GROUP_TILES])
        gate_rms = sb("gate_rms", [P, GROUP_TILES])
        gate_max = sb("gate_max", [P, GROUP_TILES])
        gate_tanh = sb("gate_tanh", [P, GROUP_TILES, EXPERTS])
        gate_sum = sb("gate_sum", [P, GROUP_TILES])
        gate_half = sb("gate_half", [P, GROUP_TILES])

        sq = sb("sq", [P, GROUP_TILES, 2 * INNER])
        ss = sb("ss", [P, GROUP_TILES, 2 * HEADS])
        seed = sb("seed", [P, GROUP_TILES, 2 * HEADS], mybir.dt.int32)
        rnorm = sb("rnorm", [P, GROUP_TILES, 2 * HEADS])
        newton = sb("newton", [P, GROUP_TILES, 2 * HEADS])
        qk_raw = sb("qk_raw", [P, GROUP_TILES, 2 * INNER])
        qkn = sb("qkn", [P, 2, GROUP_TILES * HEADS, HEAD_DIM])
        q_stack = sb("q_stack", [P, GROUP_TILES * HEADS, ROW], f16)
        k_stack = sb("k_stack", [P, GROUP_TILES * HEADS, ROW], f16)
        qT = sb("qT", [P, QUADS, TOKENS], f16)
        kT = sb("kT", [P, QUADS, GROUP], f16)
        kT_wide = [w_raw[:, :].bitcast(f16).rearrange("p (j t) -> p j t", j=4), sb("kT_wide1", [P, 4, TOKENS], f16)]
        v_ones = sb("v_ones", [P, TILES, HEADS, ROW])
        probs = sb("probs", [P, P_SLOTS, 2, GROUP])
        oT = sb("oT", [P, GROUP])
        rden = sb("rden", [P, GROUP_TILES, 4])
        o_tok = sb("o_tok", [P, GROUP_TILES, INNER])
        o_feat = sb("o_feat", [INNER, GROUP])

        ps = ctx.enter_context(nc.psum_tensor("ps", [P, 8, GROUP], f32))

        x_in = [sem(f"x_in{g}") for g in range(GROUPS)]
        small_in, b2_in, rows_in, wqkv_in, wout_in = (sem(n) for n in ("small_in", "b2_in", "rows_in", "wqkv_in", "wout_in"))
        w1_in = [sem(f"w1_in{k}") for k in range(4)]
        w2_in = [sem(f"w2_in{k}") for k in range(4)]
        out_stored = sem("out_stored")
        const_self, const_ready = sem("const_self"), sem("const_ready")
        small_t, cols_ready = sem("small_t"), sem("cols_ready")
        w1_hi_ready, w1_ready = sem("w1_hi_ready"), sem("w1_ready")
        w2_hi_ready, w2_ready = sem("w2_hi_ready"), sem("w2_ready")
        bn_done, mv_done, var_done, rstd_done, xn_done, ln_t, xf_done = (
            [sem(f"{n}_{kind}") for kind in ("ffn", "att")]
            for n in ("bn_done", "mv_done", "var_done", "rstd_done", "xn_done", "ln_t", "xf_done"))
        hi_done, xT_ready = sem("hi_done"), sem("xT_ready")
        gate_mm, gate_logits_done, gate_self, gate_rms_done, gate_shifted, gate_tanh_done, gate_ready = (
            sem(n) for n in ("gate_mm", "gate_logits_done", "gate_self", "gate_rms_done", "gate_shifted", "gate_tanh_done",
                             "gate_ready"))
        up_done, gelu_done, h_hi_done, split_done, down_done = (
            sem(n) for n in ("up_done", "gelu_done", "h_hi_done", "split_done", "down_done"))
        y_evac, y_t, resid = sem("y_evac"), sem("y_t"), sem("resid")
        qkv_mm, qkv_copied, sq_done, seed_done, newton_done, qkn_done, hi16_done, stack_done, stack_t, qT_done, kT_done = (
            sem(n) for n in ("qkv_mm", "qkv_copied", "sq_done", "seed_done", "newton_done", "qkn_done", "hi16_done",
                             "stack_done", "stack_t", "qT_done", "kT_done"))
        k_spread = [[sem(f"k_spread{p}_{quad}") for quad in range(QUADS)] for p in range(GROUPS)]
        scores_done, exp_done, mask_done, pv_done = (sem(n) for n in ("scores_done", "exp_done", "mask_done", "pv_done"))
        o_copied, rden_done = sem("o_copied"), sem("rden_done")
        job_filled, job_emptied = sem("job_filled"), sem("job_emptied")

        units = [(b, qg, quad) for b in range(BATCH) for qg in range(Q_GROUPS) for quad in range(QUADS)]
        steps = []
        for u, (b, qg, quad) in enumerate(units):
            items = score_items(qg)
            for k, item in enumerate(items):
                for pair in range(2):
                    steps.append(dict(unit=u, b=b, qg=qg, quad=quad, pair=pair, item=item, first=(k == 0),
                                      last=(k == len(items) - 1), local=k,
                                      diagonal=any(kt >= GROUP_TILES * qg for kt, *_ in item)))
        masks_until, n_masks = [], 0
        for st in steps:
            n_masks += len(st["item"]) if st["diagonal"] else 0
            masks_until.append(n_masks)
        quad_steps = len(steps) // 2
        quads_until_unit = [max(i for i, st in enumerate(steps) if st["unit"] == u) // 2 + 1 for u in range(len(units))]
        last_quad = [n - 1 for n in quads_until_unit]
        halves = ((0, 1), (2, 3))
        NEWTON_OPS, SEED_OPS = 12, 4

        u0, u1, u2, u3 = last_quad[0:4]
        LAST = GROUPS - 1
        jobs = [(u0 + 1, "rows", 0), (u0 + 2, "q_stack", LAST - 1), (u0 + 3, "k_stack", LAST - 1),
                (u1 + 1, "rows", 1), (u1 + 2, "features", 1), (u1 + 3, "project", 1),
                (u1 + 4, "ln", LAST), (u1 + 5, "qk", LAST), (u1 + 6, "v", LAST), (u2 + 4, "rows", 2),
                (u2 + 5, "q_stack", LAST), (u2 + 6, "k_stack", LAST)]
        for u in range(3, len(units) - 1):
            at = last_quad[u] + 1
            jobs.append((at, "rows", u))
            if u % 2:
                jobs += [(at + 1, "features", u), (at + 2, "project", u)]
        jobs.append((last_quad[4] + 2, "ffn_ln", 0))
        jobs.sort(key=lambda j: j[0])
        u = len(units) - 1
        jobs += [(quad_steps, "rows", u), (quad_steps, "features", u), (quad_steps, "project", u)]
        assert len({at for at, *_ in jobs}) == len(jobs) - 2
        job_number = {(kind, arg): n for n, (_, kind, arg) in enumerate(jobs)}

        def output_bank(u):
            return 7 - u % 2

        def job_bank(n):
            at = jobs[n][0]
            return 13 - output_bank(steps[2 * min(at, quad_steps - 1)]["unit"])

        def ffn_groups(eng, layer, group):
            group(0)
            if layer == 0:
                for g in range(1, GROUPS - 1):
                    group(g)
            else:
                with eng.Fori(1, GROUPS - 1) as g:
                    group(g)
            group(GROUPS - 1)

        def qkv_banks(p):
            return (BANK_LN, BANK_QT) if p == LAST - 1 else (BANK_QT, BANK_KT)

        def inverse_lengths(eng, p):
            eng.wait_ge(seed_done, SEED_OPS * p + SEED_OPS)
            for step in range(3):
                done = NEWTON_OPS * p + 4 * step
                if done:
                    eng.wait_ge(newton_done, done)
                eng.tensor_tensor(newton[:, :, :], rnorm[:, :, :], rnorm[:, :, :], ALU.mult).then_inc(newton_done, 1)
                eng.wait_ge(newton_done, done + 1)
                eng.tensor_tensor(newton[:, :, :], newton[:, :, :], ss[:, :, :], ALU.mult).then_inc(newton_done, 1)
                eng.wait_ge(newton_done, done + 2)
                eng.tensor_scalar(newton[:, :, :], newton[:, :, :], -0.5, 1.5, ALU.mult, ALU.add).then_inc(newton_done, 1)
                eng.wait_ge(newton_done, done + 3)
                eng.tensor_tensor(rnorm[:, :, :], rnorm[:, :, :], newton[:, :, :], ALU.mult).then_inc(newton_done, 1)

        def low_features(eng, g):
            part = ds(g * GROUP, GROUP)
            eng.tensor_tensor(xT_lo[:, part], xf[:, FFN, :], xT_hi[:, part].bitcast(f32), ALU.subtract).then_inc(xT_ready, 1)

        def unit_vectors(eng, p):
            if p < LAST:
                eng.wait_ge(qkv_copied, p + 1)
            else:
                eng.wait_ge(job_emptied, job_number["qk", p] + 1)
            if p:
                eng.wait_ge(stack_done, 2 * p)
            eng.wait_ge(newton_done, NEWTON_OPS * (p + 1))
            for which in range(2):
                eng.tensor_tensor(
                    qkn[:, which, :, :].rearrange("p (t h) d -> p t h d", t=GROUP_TILES),
                    qk_raw[:, :, INNER * which:INNER * which + INNER].rearrange("p t (h d) -> p t h d", h=HEADS),
                    rnorm[:, :, HEADS * which:HEADS * which + HEADS].unsqueeze(3)
                    .to_broadcast([P, GROUP_TILES, HEADS, HEAD_DIM]), ALU.mult).then_inc(qkn_done, 1)

        def high_parts():
            return ((q_stack[:, :, 0:2 * HEAD_DIM].rearrange("p h (a d) -> p h a d", a=2), 0),
                    (k_stack[:, :, :].rearrange("p h (a b d) -> p h a b d", a=2, b=2)[:, :, :, 0, :], 1))

        def twice(which):
            return qkn[:, which, :, :].unsqueeze(2).to_broadcast([P, GROUP_TILES * HEADS, 2, HEAD_DIM])

        def low_parts(eng, p):
            eng.wait_ge(hi16_done, 2 * p + 2)
            for stack, which, at in ((q_stack, 0, 2 * HEAD_DIM), (k_stack, 1, HEAD_DIM)):
                eng.tensor_tensor(stack[:, :, at:at + HEAD_DIM], qkn[:, which, :, :], stack[:, :, 0:HEAD_DIM],
                                  ALU.subtract).then_inc(stack_done, 1)

        block = ctx.enter_context(nc.Block())

        @block.sync
        def _(sp):
            w1_v = w1.rearrange("e d h -> d e h")
            w2_v = w2.rearrange("e (c p) d -> p (e c) d", p=P)
            sp.dma_start(x_sb[:, 0:4, :], x_d[:, 0:4, :]).then_inc(x_in[0], 16)

            def load_w1(k):
                sp.dma_start(w1_raw[:, 512 * k:512 * k + 512].rearrange("d (e h) -> d e h", e=2),
                             w1_v[:, 2 * k:2 * k + 2, :]).then_inc(w1_in[k], 16)

            def load_w2(k):
                sp.dma_start(w2_raw[:, 512 * k:512 * k + 512].rearrange("p (c d) -> p c d", c=4),
                             w2_v[:, 4 * k:4 * k + 4, :]).then_inc(w2_in[k], 16)

            load_w1(0)
            sp.dma_start(small[0:CHUNKS, :], b1.rearrange("e (c p) -> (e c) p", p=P)).then_inc(small_in, 16)
            sp.dma_start(small[CHUNKS:CHUNKS + 1, :], ln_w.unsqueeze(0)).then_inc(small_in, 16)
            sp.dma_start(small[CHUNKS + 1:CHUNKS + 2, :], ln_b.unsqueeze(0)).then_inc(small_in, 16)
            sp.dma_start(small[CHUNKS + 2:SMALL, :], gate_w).then_inc(small_in, 16)
            sp.dma_start(b2_sb[:, :], b2).then_inc(b2_in, 16)
            load_w2(0)
            load_w1(1)
            load_w2(1)
            load_w1(2)
            sp.dma_start(gate_b_row[:, :], gate_b.partition_broadcast(P)).then_inc(rows_in, 16)
            sp.dma_start(rms_w_row[:, :], rms_w.partition_broadcast(P)).then_inc(rows_in, 16)
            load_w2(2)
            load_w1(3)
            load_w2(3)
            for g in range(1, GROUPS):
                sp.dma_start(x_sb[:, 4 * g:4 * g + 4, :], x_d[:, 4 * g:4 * g + 4, :]).then_inc(x_in[g], 16)
            sp.dma_start(wqkv_sb[:, :], w_qkv).then_inc(wqkv_in, 16)
            sp.dma_start(wout_sb[:, :], w_out).then_inc(wout_in, 16)
            for p in range(GROUPS):
                sp.wait_ge(const_ready, 4)
                if p < GROUPS // 2:
                    sp.wait_ge(kT_done, p + 1)
                else:
                    sp.wait_ge(job_emptied, job_number["k_stack", p] + 1)
                for quad in range(QUADS):
                    for j in range(4):
                        rows = slice(ROW * j, ROW * j + ROW)
                        sp.dma_start(kT_wide[quad][rows, j, GROUP * p:GROUP * p + GROUP],
                                     kT[rows, quad, :]).then_inc(k_spread[p][quad], 16)
            for g in range(GROUPS):
                for tiles in (halves if g == LAST else (range(GROUP_TILES),)):
                    t0, t1 = 4 * g + tiles[0], 4 * g + tiles[-1] + 1
                    sp.wait_ge(resid, GROUP_TILES * GROUPS + t1)
                    sp.dma_start(out_d[:, t0:t1, :], x_sb[:, t0:t1, :]).then_inc(out_stored, 16)
            sp.wait_ge(out_stored, 16 * (GROUPS + 1))

        @block.tensor
        def _(pe):
            def ln_transpose(kind, n, others):
                at_start = isinstance(n, int) and n == 0 and kind == FFN
                if not at_start:
                    pe.wait_ge(xn_done[kind], GROUP_TILES * n + GROUP_TILES)
                pe.wait_ge(xf_done[kind], n)
                pe.wait_ge(xf_done[1 - kind], others)
                for i in range(GROUP_TILES):
                    if at_start:
                        pe.wait_ge(xn_done[kind], i + 1)
                    m = pe.transpose(ps[:, BANK_LN, P * i:P * i + P], xn[:, kind, i, :], ident[:, :])
                m.then_inc(ln_t[kind], 1)

            def gate_product(F):
                pe.wait_ge(xf_done[FFN], F + 1)
                pe.wait_ge(gate_logits_done, F)
                for i in range(GROUP_TILES):
                    m = pe.matmul(ps[:, BANK_GATE, EXPERTS * i:EXPERTS * i + EXPERTS], xf[:, FFN, P * i:P * i + P],
                                  cols[:, COL_GATE:COL_GATE + EXPERTS], start=True, stop=True)
                m.then_inc(gate_mm, 1)

            def up(F, c, g):
                n = CHUNKS * F + c
                if not (isinstance(n, int) and n < RING):
                    pe.wait_ge(gelu_done, n - RING + 1)
                bank = ps[:, BANK_H + c % RING, :]
                w = slice(P * c, P * c + P)
                cols_g = ds(g * GROUP, GROUP)
                pe.matmul(bank, w1_hi[:, w], xT_hi[:, cols_g], start=True, stop=False)
                pe.matmul(bank, w1_hi[:, w], xT_lo[:, cols_g], start=False, stop=False)
                pe.matmul(bank, w1_lo[:, w], xT_hi[:, cols_g], start=False, stop=True).then_inc(up_done, 1)

            def down(F, c):
                pe.wait_ge(split_done, CHUNKS * F + c + 1)
                if isinstance(F, int) and F == 0 and c % 4 == 0:
                    pe.wait_ge(w2_ready, c // 4 + 1)
                w = slice(P * c, P * c + P)
                y = ps[:, BANK_Y, :]
                pe.matmul(y, w2_hi[:, w], h_hi[:, c % RING, :], start=(c == 0), stop=False)
                pe.matmul(y, w2_hi[:, w], h_lo[:, c % RING, :], start=False, stop=False)
                pe.matmul(y, w2_lo[:, w], h_hi[:, c % RING, :], start=False, stop=(c == CHUNKS - 1)).then_inc(down_done, 1)

            def y_transposes(F, bank=BANK_YT, ln_groups=GROUPS, att_groups=LAST):
                pe.wait_ge(y_evac, F + 1)
                if bank == BANK_LN:
                    pe.wait_ge(xf_done[FFN], ln_groups)
                    pe.wait_ge(xf_done[ATT], att_groups) if att_groups else None
                else:
                    pe.wait_ge(qkv_copied, LAST)
                for i in range(GROUP_TILES):
                    m = pe.transpose(ps[:, bank, P * i:P * i + P], yT[:, P * i:P * i + P], ident[:, :])
                m.then_inc(y_t, 1)

            def ffn_group(layer, g):
                F = GROUPS * layer + g
                last = isinstance(g, int) and g == LAST
                first = isinstance(g, int) and g == 0
                operands = layer == 0
                for c in range(CHUNKS):
                    if c:
                        down(F, c)
                    if c + LAG < CHUNKS:
                        if layer == 0 and g == 0 and (c + LAG) % 4 == 0:
                            pe.wait_ge(w1_ready, (c + LAG) // 4 + 1)
                        up(F, c + LAG, g)
                    elif not last:
                        if c + LAG == CHUNKS:
                            pe.wait_ge(xT_ready, F + 2)
                        up(F + 1, c + LAG - CHUNKS, g + 1)
                    if c == 0:
                        if layer or not first:
                            pe.wait_ge(y_evac, F)
                        down(F, 0)
                        if not first:
                            y_transposes(F - 1, ln_groups=F + 1, att_groups=g - 1 if operands else LAST)
                    if layer == 1 and first and c in (2, 4, 6):
                        fill(len(jobs) - 4 + c // 2)
                    if c == (8 if layer == 1 and first else 3):
                        if operands and g >= 3:
                            pe.wait_ge(kT_done, g - 2)
                        if operands and g >= 2:
                            pe.wait_ge(qkv_copied, g - 1)
                        if layer == 1 and first:
                            pe.wait_ge(job_emptied, len(jobs))
                        gate_product(F)
                    if operands and last and c == 13:
                        pe.wait_ge(qT_done, 1)
                        pe.wait_ge(k_spread[0][0], 64)
                        pe.wait_ge(gelu_done, CHUNKS * GROUPS - 2)
                        scores(0)
                    if c == 9 and not last:
                        if layer or not first:
                            pe.wait_ge(resid, GROUP_TILES * F)
                        ln_transpose(FFN, F + 1, max(g - 1, 0) if layer == 0 else LAST)
                    if operands and c == 12 and g >= 2:
                        stack_transposes(g - 2)
                    if operands and g >= 1 and c == (11 if last else 14):
                        pe.wait_ge(resid, GROUP_TILES * F)
                        ln_transpose(ATT, g - 1, min(g + 2, GROUPS))
                    if operands and g >= 1 and c == (14 if last else 15):
                        qkv_products(g - 1)

            def qkv_products(p):
                if p == 0:
                    pe.wait_ge(wqkv_in, 16)
                pe.wait_ge(xf_done[ATT], p + 1)
                if p == LAST - 1:
                    pe.wait_ge(qT_done, p)
                else:
                    pe.wait_ge(gate_logits_done, p + 2)
                    pe.wait_ge(qT_done, p)
                    pe.wait_ge(kT_done, p)
                for i in range(GROUP_TILES):
                    m = pe.matmul(ps[:, qkv_banks(p)[i // 2], 192 * (i % 2):192 * (i % 2) + 192], xf[:, ATT, P * i:P * i + P],
                                  wqkv_sb[:, :], start=True, stop=True)
                m.then_inc(qkv_mm, 1)

            def transpose_stack(stack, bank):
                dst = ps[:, bank, :].bitcast(f16)
                for quad in range(QUADS):
                    for i in range(GROUP_TILES):
                        src = stack[:, HEADS * i + 4 * quad:HEADS * i + 4 * quad + 4, :].rearrange("p h r -> p (h r)")
                        m = pe.transpose(dst[:, GROUP * quad + P * i:GROUP * quad + P * i + P], src, ident16[:, :])
                return m

            def stack_transposes(p):
                pe.wait_ge(stack_done, 2 * p + 2)
                pe.wait_ge(qkv_copied, p + 1)
                pe.wait_ge(gate_logits_done, p + 3)
                pe.wait_ge(qT_done, p)
                pe.wait_ge(kT_done, p)
                transpose_stack(q_stack, BANK_QT)
                transpose_stack(k_stack, BANK_KT).then_inc(stack_t, 1)

            def scores(s):
                st = steps[s]
                if s >= S_SETS:
                    pe.wait_ge(exp_done, s - S_SETS + 1)
                for hd in range(2):
                    j = 2 * st["pair"] + hd
                    bank = 2 * (s % S_SETS) + hd
                    for kt, q0, width, at in st["item"]:
                        k0 = SEQ * st["b"] + P * kt
                        qc = SEQ * st["b"] + GROUP * st["qg"] + q0
                        m = pe.matmul(ps[:, bank, at:at + width], kT_wide[st["quad"]][:, j, k0:k0 + P],
                                      qT[:, st["quad"], qc:qc + width], start=True, stop=True)
                m.then_inc(scores_done, 1)

            def pv(k):
                s = 2 * k
                st = steps[s]
                bank = output_bank(st["unit"])
                if st["first"] and st["unit"] == 0:
                    pe.wait_ge(kT_done, LAST - 1)
                if st["first"] and st["unit"] == 1:
                    pe.wait_ge(resid, GROUP_TILES * GROUPS)
                if st["first"] and st["unit"] > 1:
                    pe.wait_ge(job_emptied, sum(at < k for at, *_ in jobs))
                if st["diagonal"]:
                    pe.wait_ge(mask_done, masks_until[s + 1])
                else:
                    pe.wait_ge(exp_done, s + 2)
                for n, (kt, q0, width, at) in enumerate(st["item"]):
                    for j in range(4):
                        m = pe.matmul(ps[ROW * j:ROW * j + ROW, bank, q0:q0 + width],
                                      v_ones[:, SEQ // P * st["b"] + kt, 4 * st["quad"] + j, :],
                                      probs[:, (s + j // 2) % P_SLOTS, j % 2, at:at + width],
                                      start=(st["first"] and n == 0), stop=(st["last"] and n == len(st["item"]) - 1))
                m.then_inc(pv_done, 1)

            def fill(n):
                _, kind, arg = jobs[n]
                bank = ps[:, job_bank(n), :]
                if n:
                    pe.wait_ge(job_emptied, n)
                tiles = [slice(P * i, P * i + P) for i in range(GROUP_TILES)]
                if kind in ("q_stack", "k_stack"):
                    pe.wait_ge(stack_done, 2 * arg + 2)
                    m = transpose_stack(q_stack if kind == "q_stack" else k_stack, job_bank(n))
                elif kind in ("ln", "ffn_ln"):
                    norm = ATT if kind == "ln" else FFN
                    pe.wait_ge(xn_done[norm], GROUP_TILES * (LAST + 1 if kind == "ln" else GROUPS + 1))
                    for i, tile in enumerate(tiles):
                        m = pe.transpose(bank[:, tile], xn[:, norm, i, :], ident[:, :])
                elif kind == "qk":
                    for tile in tiles:
                        m = pe.matmul(bank[:, tile], xf[:, ATT, tile], wqkv_sb[:, 0:2 * INNER], start=True, stop=True)
                elif kind == "v":
                    for i, tile in enumerate(tiles):
                        m = pe.matmul(bank[:, INNER * i:INNER * i + INNER], xf[:, ATT, tile],
                                      wqkv_sb[:, 2 * INNER:3 * INNER], start=True, stop=True)
                elif kind == "rows":
                    pe.wait_ge(o_copied, arg + 1)
                    for tile in tiles:
                        m = pe.transpose(bank[:, tile], oT[:, tile], ident[:, :])
                elif kind == "features":
                    for i, tile in enumerate(tiles):
                        m = pe.transpose(bank[0:INNER, tile], o_tok[:, i, :], ident[:, :])
                elif kind == "project":
                    for tile in tiles:
                        m = pe.matmul(bank[:, tile], o_feat[:, tile], wout_sb[:, :], start=True, stop=True)
                m.then_inc(job_filled, 1)

            pe.wait_ge(const_self, 1)
            for _ in range(WARM_UP):
                pe.matmul(ps[:, BANK_H + RING - 1, 0:P], ones[:, :], ones[:, :], start=True, stop=True)
            pe.wait_ge(const_ready, 1)
            pe.wait_ge(small_in, 64)
            pe.transpose(ps[:, BANK_GATE, 0:SMALL], small[:, :], ident[0:SMALL, 0:SMALL])
            pe.wait_ge(b2_in, 16)
            pe.matmul(ps[:, BANK_GATE, COL_B2:COL_B2 + 1], b2_sb[:, :], ones[0:EXPERTS, 0:1],
                      start=True, stop=True).then_inc(small_t, 1)
            ln_transpose(FFN, 0, 0)
            pe.wait_ge(xT_ready, 1)
            pe.wait_ge(w1_ready, 1)
            for c in range(LAG):
                up(0, c, 0)
            ffn_groups(nc.tensor, 0, lambda g: ffn_group(0, g))

            pe.wait_ge(qT_done, 2)
            pe.wait_ge(wout_in, 16)
            next_job = 0
            for k in range(quad_steps + PV_LAG):
                if k < quad_steps:
                    st = steps[2 * k]
                    if st["first"]:
                        p = Q_GROUPS * st["b"] + st["qg"]
                        pe.wait_ge(k_spread[p][st["quad"]], 64)
                        if st["b"]:
                            pe.wait_ge(job_emptied, job_number["q_stack", p] + 1)
                    for s in (2 * k, 2 * k + 1):
                        if s == 0:
                            continue
                        if s < S_SETS:
                            if s == 1:
                                pe.wait_ge(gelu_done, CHUNKS * GROUPS)
                            else:
                                pe.wait_ge(qkv_copied, LAST)
                                pe.wait_ge(y_evac, GROUPS)
                                pe.wait_ge(xf_done[FFN], GROUPS)
                        scores(s)
                    if k == 0:
                        y_transposes(LAST, BANK_YT_LAST)
                if k >= PV_LAG:
                    if k == quad_steps + PV_LAG - 1:
                        pe.wait_ge(xT_ready, GROUPS + 1)
                        for c in range(LAG):
                            pe.wait_ge(exp_done, len(steps) - 2 + c // 2 + 1)
                            up(GROUPS, c, 0)
                    pv(k - PV_LAG)
                    if jobs[next_job][0] == k - PV_LAG:
                        fill(next_job)
                        next_job += 1
            ffn_groups(nc.tensor, 1, lambda g: ffn_group(1, g))
            for half, bank in enumerate((BANK_YT, BANK_YT_LAST)):
                pe.wait_ge(y_evac, 2 * GROUPS + half)
                if half == 0:
                    pe.wait_ge(xf_done[FFN], 2 * GROUPS)
                for i in halves[half]:
                    m = pe.transpose(ps[:, bank, P * i:P * i + P], yT[:, P * i:P * i + P], ident[:, :])
                m.then_inc(y_t, 1)

        @block.scalar
        def _(act):
            def ffn_features(layer, F, g):
                act.wait_ge(ln_t[FFN], F + 1 - layer)
                act.wait_ge(xT_ready, F)
                act.wait_ge(gate_mm, F)
                nc.scalar.activation(xf[:, FFN, :], ps[:, BANK_LN, :], ACT.Copy).then_inc(xf_done[FFN], 1)
                act.wait_ge(xf_done[FFN], F + 1)
                nc.scalar.activation(xT_hi[:, ds(g * GROUP, GROUP)], xf[:, FFN, :], ACT.Copy).then_inc(hi_done, 1)

            def affine_features(p):
                act.wait_ge(ln_t[ATT], p + 1)
                act.wait_ge(qkv_mm, p)
                nc.scalar.activation(xf[:, ATT, :], ps[:, BANK_LN, :], ACT.Identity, bias=cols[:, COL_LNB:COL_LNB + 1],
                                     scale=cols[:, COL_LNW:COL_LNW + 1]).then_inc(xf_done[ATT], 1)

            def qkv_halves(p):
                return [(half, ps[:, qkv_banks(p)[half], 0:384].rearrange("p (t c) -> p t c", t=2)) for half in range(2)]

            def square_qk(p):
                act.wait_ge(qkv_mm, p + 1)
                act.wait_ge(seed_done, SEED_OPS * p)
                for half, qkv in qkv_halves(p):
                    nc.scalar.activation(sq[:, 2 * half:2 * half + 2, :], qkv[:, :, 0:2 * INNER], ACT.Square).then_inc(sq_done, 1)

            def copy_qkv(p):
                act.wait_ge(qkn_done, 2 * p)
                for half, qkv in qkv_halves(p):
                    nc.scalar.activation(qk_raw[:, 2 * half:2 * half + 2, :], qkv[:, :, 0:2 * INNER], ACT.Copy)
                if p == 0:
                    act.wait_ge(const_ready, 3)
                for half, qkv in qkv_halves(p):
                    last = nc.scalar.activation(v_ones[:, 4 * p + 2 * half:4 * p + 2 * half + 2, :, 0:HEAD_DIM],
                                                qkv[:, :, 2 * INNER:3 * INNER].rearrange("p t (h d) -> p t h d", h=HEADS),
                                                ACT.Copy)
                last.then_inc(qkv_copied, 1)

            def copy_k(p):
                act.wait_ge(stack_t, p + 1)
                if p:
                    for spread in k_spread[p - 1]:
                        act.wait_ge(spread, 64)
                nc.scalar.activation(kT[:, :, :],
                                     ps[:, BANK_KT, :].bitcast(f16).rearrange("p (a q) -> p a q", a=QUADS),
                                     ACT.Copy).then_inc(kT_done, 1)

            def high_stacks(p):
                act.wait_ge(qkn_done, 2 * p + 2)
                if p:
                    act.wait_ge(stack_t, p)
                for dst, which in high_parts():
                    nc.scalar.activation(dst, twice(which), ACT.Copy).then_inc(hi16_done, 1)

            def gate_tanh_of(F):
                act.wait_ge(gate_shifted, F + 1)
                nc.scalar.activation(gate_tanh[:, :, :], gate_tmp[:, :, :], ACT.Tanh, scale=-1.0).then_inc(gate_tanh_done, 1)

            def gelu(F, c):
                n = CHUNKS * F + c
                act.wait_ge(up_done, n + 1)
                slot = c % RING
                bias = cols[:, COL_B1 + c:COL_B1 + c + 1]
                if not (isinstance(n, int) and n < RING):
                    act.wait_ge(split_done, n - RING + 1)
                    act.wait_ge(down_done, n - RING + 1)
                first = nc.scalar.activation(h[:, slot, :], ps[:, BANK_H + slot, :], ACT.Gelu, bias=bias)
                if c % 2 == 0:
                    nc.scalar.activation(h_hi[:, slot, :], ps[:, BANK_H + slot, :], ACT.Gelu, bias=bias).then_inc(gelu_done, 1)
                else:
                    first.then_inc(gelu_done, 1)

            def exp_scores(s):
                act.wait_ge(scores_done, s + 1)
                if s >= P_SLOTS:
                    act.wait_ge(pv_done, (s - P_SLOTS) // 2 + 1)
                width = sum(w for _, _, w, _ in steps[s]["item"])
                bank = 2 * (s % S_SETS)
                nc.scalar.activation(probs[:, s % P_SLOTS, :, 0:width], ps[:, bank:bank + 2, 0:width], ACT.Exp,
                                     scale=SCALE).then_inc(exp_done, 1)

            def evacuate_y(F):
                act.wait_ge(down_done, CHUNKS * F + CHUNKS)
                if not (isinstance(F, int) and F == 0):
                    act.wait_ge(y_t, F)
                at_end = isinstance(F, int) and F == 2 * GROUPS - 1
                width = GROUP // 2 if at_end else GROUP
                for q0 in range(0, GROUP, width):
                    nc.scalar.activation(yT[:, q0:q0 + width], ps[:, BANK_Y, q0:q0 + width], ACT.Identity,
                                         bias=cols[:, COL_B2:COL_B2 + 1]).then_inc(y_evac, 1)

            def ffn_group(layer, g):
                F = GROUPS * layer + g
                last = isinstance(g, int) and g == GROUPS - 1
                first = isinstance(g, int) and g == 0
                operands = layer == 0
                for c in range(CHUNKS):
                    if layer == 0 and first and c in (0, 2):
                        weight_hi(2 + c // 2)
                    if operands and last and c == CHUNKS - LAG + 1:
                        nc.scalar.activation(table_use[:, 1:2], ones[:, 0:1], ACT.Exp)
                    if operands and c == CHUNKS - 1 and last:
                        exp_scores(0)
                        square_qk(g - 1)
                        copy_qkv(g - 1)
                    if c == CHUNKS - 1:
                        evacuate_y(F)
                    if c + LAG < CHUNKS:
                        gelu(F, c + LAG)
                    elif not last:
                        gelu(F + 1, c + LAG - CHUNKS)
                    if operands and g >= 2:
                        if c == 0:
                            square_qk(g - 2)
                        if c == 1:
                            copy_qkv(g - 2)
                        if c == 9:
                            high_stacks(g - 2)
                        if c == 13:
                            copy_k(g - 2)
                    if operands and g >= 1 and c == (12 if last else 14):
                        affine_features(g - 1)
                    if c == 9 and not last:
                        ffn_features(layer, F + 1, g + 1)
                    if c == (12 if layer == 1 and first else 10):
                        gate_tanh_of(F)
            def weight_hi(k):
                part = slice(512 * k, 512 * k + 512)
                act.wait_ge(w2_in[k], 16)
                nc.scalar.activation(w2_hi[:, part], w2_raw[:, part], ACT.Copy).then_inc(w2_hi_ready, 1)

            act.wait_ge(const_self, 3)
            nc.scalar.activation(table_use[:, 0:1], ones[:, 0:1], ACT.Gelu)
            weight_hi(0)
            act.wait_ge(ln_t[FFN], 1)
            nc.scalar.activation(xT_hi[:, 0:GROUP], ps[:, BANK_LN, :], ACT.Copy).then_inc(hi_done, 1)
            act.wait_ge(xT_ready, 1)
            nc.scalar.activation(xf[:, FFN, :], ps[:, BANK_LN, :], ACT.Copy).then_inc(xf_done[FFN], 1)
            weight_hi(1)
            act.wait_ge(cols_ready, 1)
            for c in range(LAG):
                gelu(0, c)
            ffn_groups(nc.scalar, 0, lambda g: ffn_group(0, g))
            for s in range(1, len(steps)):
                exp_scores(s)
            for c in range(LAG):
                gelu(GROUPS, c)
            ffn_groups(nc.scalar, 1, lambda g: ffn_group(1, g))

        @block.vector
        def _(dve):
            def x_tile(g, i):
                return x_sb[:, ds(4 * g + i, 1), :].rearrange("p a d -> p (a d)")

            def stats(kind, g, tiles):
                for i in tiles:
                    dve.bn_stats(bn_part[:, kind, i, :], x_tile(g, i)).then_inc(bn_done[kind], 1)

            def wait_stats(kind, n):
                dve.wait_ge(bn_done[kind], GROUP_TILES * n + GROUP_TILES)
                dve.wait_ge(rstd_done[kind], n)

            def aggregate(kind):
                for i in range(GROUP_TILES):
                    dve.bn_aggr(mean_var[:, kind, i, :], bn_part[:, kind, i, :]).then_inc(mv_done[kind], 1)

            def normalise(kind, n, g, tiles=range(GROUP_TILES), jobs_before=0):
                dve.wait_ge(rstd_done[kind], n + 1)
                dve.wait_ge(ln_t[kind], n - jobs_before)
                for i in tiles:
                    dve.tensor_scalar(xn[:, kind, i, :], x_tile(g, i), mean_var[:, kind, i, 0:1], rstd[:, kind, i:i + 1],
                                      ALU.subtract, ALU.mult).then_inc(xn_done[kind], 1)

            def per_tile(v):
                return v.unsqueeze(2).to_broadcast([P, GROUP_TILES, EXPERTS])

            def per_expert(v):
                return v.unsqueeze(1).to_broadcast([P, GROUP_TILES, EXPERTS])

            def gate_logits(F):
                dve.wait_ge(gate_mm, F + 1)
                dve.tensor_tensor(logits[:, :, :], ps[:, BANK_GATE, 0:GROUP_TILES * EXPERTS].rearrange("p (t e) -> p t e", e=EXPERTS),
                                  per_expert(gate_b_row[:, :]), ALU.add).then_inc(gate_logits_done, 1)
                dve.wait_ge(gate_logits_done, F + 1)
                dve.tensor_tensor(gate_tmp[:, :, :], logits[:, :, :], logits[:, :, :], ALU.mult).then_inc(gate_self, 1)
                dve.wait_ge(gate_self, 6 * F + 1)
                dve.tensor_reduce(gate_ms[:, :], gate_tmp[:, :, :], AX.X, ALU.add).then_inc(gate_self, 1)
                dve.wait_ge(gate_self, 6 * F + 2)
                dve.tensor_scalar(gate_ms[:, :], gate_ms[:, :], 1.0 / EXPERTS, RMS_EPS, ALU.mult, ALU.add).then_inc(gate_self, 1)

            def gate_shift(F):
                dve.wait_ge(gate_rms_done, F + 1)
                dve.tensor_tensor(gate_tmp[:, :, :], logits[:, :, :], per_tile(gate_rms[:, :]), ALU.mult).then_inc(gate_self, 1)
                dve.wait_ge(gate_self, 6 * F + 4)
                dve.tensor_tensor(logits[:, :, :], gate_tmp[:, :, :], per_expert(rms_w_row[:, :]), ALU.mult).then_inc(gate_self, 1)
                dve.wait_ge(gate_self, 6 * F + 5)
                dve.tensor_reduce(gate_max[:, :], logits[:, :, :], AX.X, ALU.max).then_inc(gate_self, 1)
                dve.wait_ge(gate_self, 6 * F + 6)
                dve.tensor_tensor(gate_tmp[:, :, :], logits[:, :, :], per_tile(gate_max[:, :]), ALU.subtract).then_inc(gate_shifted, 1)

            def gate_weight(F):
                dve.wait_ge(gate_tanh_done, F + 1)
                dve.tensor_scalar(gate_tanh[:, :, :], gate_tanh[:, :, :], 1.0, None, ALU.add).then_inc(gate_ready, 1)
                dve.wait_ge(gate_ready, 5 * F + 1)
                dve.reciprocal(logits[:, :, :], gate_tanh[:, :, :]).then_inc(gate_ready, 1)
                dve.wait_ge(gate_ready, 5 * F + 2)
                dve.tensor_reduce(gate_sum[:, :], logits[:, :, :], AX.X, ALU.add).then_inc(gate_ready, 1)
                dve.wait_ge(gate_ready, 5 * F + 3)
                dve.tensor_scalar(gate_sum[:, :], gate_sum[:, :], 4e-6, 2.0 - 2e-6 * EXPERTS, ALU.mult, ALU.add).then_inc(gate_ready, 1)
                dve.wait_ge(gate_ready, 5 * F + 4)
                dve.reciprocal(gate_half[:, :], gate_sum[:, :]).then_inc(gate_ready, 1)

            def split(F, c):
                n = CHUNKS * F + c
                slot = c % RING
                dve.wait_ge(gelu_done, n + 1)
                if not (isinstance(n, int) and n < RING):
                    dve.wait_ge(down_done, n - RING + 1)
                if c % 2:
                    dve.tensor_copy(h_hi[:, slot, :], h[:, slot, :]).then_inc(h_hi_done, 1)
                    dve.wait_ge(h_hi_done, CHUNKS // 2 * F + (c + 1) // 2)
                dve.tensor_tensor(h_lo[:, slot, :], h[:, slot, :], h_hi[:, slot, :].bitcast(f32),
                                  ALU.subtract).then_inc(split_done, 1)

            def residual(F, g, tiles=range(GROUP_TILES), bank=BANK_YT, transposed=1):
                dve.wait_ge(y_t, F + transposed)
                dve.wait_ge(gate_ready, 5 * F + 5)
                for i in tiles:
                    xi = x_tile(g, i)
                    dve.scalar_tensor_tensor(xi, ps[:, bank, P * i:P * i + P], gate_half[:, i:i + 1], xi,
                                             ALU.mult, ALU.add).then_inc(resid, 1)

            def square_sums(p):
                dve.wait_ge(sq_done, 2 * p + 2)
                if p:
                    dve.wait_ge(newton_done, NEWTON_OPS * p)
                dve.tensor_reduce(ss[:, :, :].rearrange("p t h -> p (t h)"),
                                  sq[:, :, :].rearrange("p t (h d) -> p (t h) d", d=HEAD_DIM), AX.X, ALU.add).then_inc(seed_done, 1)

            def guesses(p):
                done = SEED_OPS * p
                dve.wait_ge(seed_done, done + 1)
                dve.tensor_scalar(ss[:, :, :], ss[:, :, :], L2_EPS, None, ALU.add).then_inc(seed_done, 1)
                dve.wait_ge(seed_done, done + 2)
                dve.tensor_scalar(seed[:, :, :], ss[:, :, :].bitcast(mybir.dt.int32), 1, None,
                                  ALU.arith_shift_right).then_inc(seed_done, 1)
                dve.wait_ge(seed_done, done + 3)
                if p:
                    dve.wait_ge(qkn_done, 2 * p)
                dve.tensor_scalar(rnorm[:, :, :].bitcast(mybir.dt.int32), seed[:, :, :], -1.0, float(0x5F3759DF),
                                  ALU.mult, ALU.add).then_inc(seed_done, 1)

            def own_squares(p):
                dve.wait_ge(job_emptied, job_number["qk", p] + 1)
                dve.tensor_tensor(sq[:, :, :], qk_raw[:, :, :], qk_raw[:, :, :], ALU.mult).then_inc(sq_done, 2)

            def stacks(p):
                dve.wait_ge(qkn_done, 2 * p + 2)
                if p == LAST:
                    dve.wait_ge(job_filled, job_number["k_stack", p - 1] + 1)
                else:
                    dve.wait_ge(stack_t, p)
                for dst, which in high_parts():
                    dve.tensor_copy(dst, twice(which)).then_inc(hi16_done, 1)
                low_parts(dve, p)

            def copy_q(p):
                dve.wait_ge(stack_t, p + 1)
                dve.tensor_copy(qT[:, :, GROUP * p:GROUP * p + GROUP],
                                ps[:, BANK_QT, :].bitcast(f16).rearrange("p (a q) -> p a q", a=QUADS)).then_inc(qT_done, 1)

            def ffn_group(layer, g):
                F = GROUPS * layer + g
                last = isinstance(g, int) and g == LAST
                first = isinstance(g, int) and g == 0
                operands = layer == 0
                for c in range(CHUNKS):
                    if c == 2 and not last:
                        wait_stats(FFN, F + 1)
                    if c + LAG < CHUNKS:
                        split(F, c + LAG)
                    elif not last:
                        split(F + 1, c + LAG - CHUNKS)
                    if layer == 0 and first and c == 0:
                        weight_parts(3)
                    if not last:
                        if c == 0:
                            if layer == 0:
                                dve.wait_ge(x_in[g + 1], 16)
                            stats(FFN, g + 1, (0, 1))
                        if c == 1:
                            stats(FFN, g + 1, (2, 3))
                        if c == 2:
                            aggregate(FFN)
                        if c in (5, 6):
                            normalise(FFN, F + 1, g + 1, halves[c - 5], jobs_before=layer)
                    if c in (1, 2) and not first:
                        residual(F - 1, g - 1, halves[c - 1])
                    if operands and g >= 1:
                        if c == 3:
                            stats(ATT, g - 1, halves[0])
                        if c == 4:
                            stats(ATT, g - 1, halves[1])
                        if c == 6:
                            wait_stats(ATT, g - 1)
                            aggregate(ATT)
                        if c in (11, 12) and not last:
                            normalise(ATT, g - 1, g - 1, halves[c - 11])
                        if c == 8 and last:
                            normalise(ATT, g - 1, g - 1)
                    if operands and g >= 2 and c == 2:
                        square_sums(g - 2)
                    if operands and g >= 2 and c == 3:
                        guesses(g - 2)
                    if operands and g >= 2 and c == 13:
                        copy_q(g - 2)
                    if operands and last and c == CHUNKS - 1:
                        square_sums(g - 1)
                        guesses(g - 1)
                    if layer == 1 and first:
                        if c == 0:
                            copy_o(len(units) - 1)
                        if c in (2, 4, 6):
                            empty(len(jobs) - 4 + c // 2)
                        if c == 7:
                            dve.wait_ge(job_emptied, len(jobs))
                    if c == (9 if layer == 1 and first else 4):
                        if layer == 0 and g == 0:
                            dve.wait_ge(rows_in, 32)
                        gate_logits(F)
                    if c == (11 if layer == 1 and first else 9):
                        gate_shift(F)
                    if c == (14 if layer == 1 and first or layer == 0 and last else 12):
                        gate_weight(F)

            def first_stats(F):
                stats(FFN, 0, range(GROUP_TILES))
                wait_stats(FFN, F)
                aggregate(FFN)

            def weight_parts(k):
                part = slice(512 * k, 512 * k + 512)
                dve.wait_ge(w1_in[k], 16)
                dve.tensor_copy(w1_hi[:, part], w1_raw[:, part]).then_inc(w1_hi_ready, 1)
                dve.wait_ge(w1_hi_ready, k + 1)
                dve.tensor_tensor(w1_lo[:, part], w1_raw[:, part], w1_hi[:, part].bitcast(f32),
                                  ALU.subtract).then_inc(w1_ready, 1)

            def copy_o(u):
                dve.wait_ge(pv_done, quads_until_unit[u])
                if u:
                    dve.wait_ge(job_filled, job_number["rows", u - 1] + 1)
                dve.tensor_copy(oT[:, :], ps[:, output_bank(u), :]).then_inc(o_copied, 1)

            def empty(n):
                _, kind, arg = jobs[n]
                bank = ps[:, job_bank(n), :]
                dve.wait_ge(job_filled, n + 1)
                if kind == "q_stack":
                    dve.tensor_copy(qT[:, :, GROUP * arg:GROUP * arg + GROUP],
                                    bank.bitcast(f16).rearrange("p (a q) -> p a q", a=QUADS)).then_inc(job_emptied, 1)
                elif kind == "k_stack":
                    for spread in k_spread[arg - 1]:
                        dve.wait_ge(spread, 64)
                    dve.tensor_copy(kT[:, :, :], bank.bitcast(f16).rearrange("p (a q) -> p a q", a=QUADS)).then_inc(job_emptied, 1)
                elif kind == "ln":
                    dve.wait_ge(qkv_mm, LAST)
                    dve.tensor_scalar(xf[:, ATT, :], bank, cols[:, COL_LNW:COL_LNW + 1], cols[:, COL_LNB:COL_LNB + 1],
                                      ALU.mult, ALU.add).then_inc(job_emptied, 1)
                elif kind == "qk":
                    dve.wait_ge(qkn_done, 2 * arg)
                    dve.tensor_copy(qk_raw[:, :, :].rearrange("p t c -> p (t c)"), bank).then_inc(job_emptied, 1)
                elif kind == "v":
                    dve.tensor_copy(v_ones[:, 4 * arg:4 * arg + 4, :, 0:HEAD_DIM],
                                    bank[:, 0:GROUP_TILES * INNER].rearrange("p (t h d) -> p t h d", t=GROUP_TILES, h=HEADS)
                                    ).then_inc(job_emptied, 1)
                elif kind == "ffn_ln":
                    dve.wait_ge(gate_mm, GROUPS)
                    dve.tensor_copy(xf[:, FFN, :], bank).then_inc(xf_done[FFN], 1)
                    dve.wait_ge(xf_done[FFN], GROUPS + 1)
                    dve.tensor_copy(xT_hi[:, 0:GROUP], bank).then_inc(job_emptied, 1)
                elif kind == "rows":
                    quad = units[arg][2]
                    rows = bank.rearrange("p (t h r) -> p t h r", t=GROUP_TILES, h=4)
                    dve.reciprocal(rden[:, :, :], rows[:, :, :, HEAD_DIM]).then_inc(rden_done, 1)
                    dve.wait_ge(rden_done, arg + 1)
                    dve.tensor_tensor(o_tok[:, :, 4 * HEAD_DIM * quad:4 * HEAD_DIM * (quad + 1)].rearrange("p t (h d) -> p t h d", h=4),
                                      rows[:, :, :, 0:HEAD_DIM],
                                      rden[:, :, :].unsqueeze(3).to_broadcast([P, GROUP_TILES, 4, HEAD_DIM]),
                                      ALU.mult).then_inc(job_emptied, 1)
                elif kind == "features":
                    dve.tensor_copy(o_feat[:, :], bank[0:INNER, :]).then_inc(job_emptied, 1)
                elif kind == "project":
                    t0 = SEQ // P * units[arg][0] + GROUP_TILES * units[arg][1]
                    xi = x_sb[:, t0:t0 + GROUP_TILES, :].rearrange("p t d -> p (t d)")
                    dve.tensor_tensor(xi, bank, xi, ALU.add).then_inc(job_emptied, 1)

            dve.wait_ge(x_in[0], 16)
            first_stats(0)
            weight_parts(0)
            normalise(FFN, 0, 0)
            dve.wait_ge(small_t, 1)
            dve.tensor_copy(cols[:, :], ps[:, BANK_GATE, 0:SMALL + 1]).then_inc(cols_ready, 1)
            dve.wait_ge(hi_done, 1)
            dve.tensor_tensor(xT_lo[:, 0:GROUP], ps[:, BANK_LN, :], xT_hi[:, 0:GROUP].bitcast(f32),
                              ALU.subtract).then_inc(xT_ready, 1)
            weight_parts(1)
            weight_parts(2)
            for c in range(LAG):
                split(0, c)
            ffn_groups(nc.vector, 0, lambda g: ffn_group(0, g))

            residual(LAST, LAST, bank=BANK_YT_LAST)
            dve.wait_ge(resid, GROUP_TILES * GROUPS)
            stats(ATT, LAST, range(GROUP_TILES))
            wait_stats(ATT, LAST)
            aggregate(ATT)
            inverse_lengths(dve, LAST - 1)
            unit_vectors(dve, LAST - 1)
            stacks(LAST - 1)
            for n, (_, kind, arg) in enumerate(jobs[:-3]):
                if kind == "ffn_ln":
                    normalise(FFN, GROUPS, 0)
                if kind == "rows":
                    copy_o(arg)
                empty(n)
                if (kind, arg) == ("rows", 0):
                    normalise(ATT, LAST, LAST)
                if kind == "v":
                    own_squares(LAST)
                    square_sums(LAST)
                    guesses(LAST)
                    inverse_lengths(dve, LAST)
                    unit_vectors(dve, LAST)
                    stacks(LAST)
                if (kind, arg) == ("project", 1):
                    dve.wait_ge(job_emptied, n + 1)
                    first_stats(GROUPS)
                if kind == "ffn_ln":
                    dve.wait_ge(job_emptied, n + 1)
                    low_features(dve, 0)
            dve.wait_ge(job_emptied, len(jobs) - 3)
            for c in range(LAG):
                split(GROUPS, c)
            ffn_groups(nc.vector, 1, lambda g: ffn_group(1, g))
            residual(2 * GROUPS - 1, LAST, halves[0])
            residual(2 * GROUPS - 1, LAST, halves[1], BANK_YT_LAST, transposed=2)

        @block.gpsimd
        def _(pool):
            def power(dst, src):
                return pool.tensor_tensor(dst, src, neg_half[:, 0:1].to_broadcast([P, GROUP_TILES]), ALU.pow)

            def add_eps(kind, src):
                pool.tensor_tensor(var_eps[:, kind, :], src, ln_eps[:, 0:1].to_broadcast([P, GROUP_TILES]),
                                   ALU.add).then_inc(var_done[kind], 1)

            def ln_once(n):
                pool.wait_ge(mv_done[FFN], GROUP_TILES * n + GROUP_TILES)
                add_eps(FFN, mean_var[:, FFN, :, 1])
                pool.wait_ge(var_done[FFN], n + 1)
                pool.wait_ge(xn_done[FFN], GROUP_TILES * n)
                power(rstd[:, FFN, :], var_eps[:, FFN, :]).then_inc(rstd_done[FFN], 1)

            def ln_twice(n):
                pool.wait_ge(mv_done[ATT], GROUP_TILES * n + GROUP_TILES)
                pool.tensor_scalar(var_eps[:, ATT, :], mean_var[:, ATT, :, 1], 1.0 + LN_EPS, LN_EPS * LN_EPS,
                                   ALU.mult, ALU.add).then_inc(var_done[ATT], 1)
                pool.wait_ge(var_done[ATT], n + 1)
                pool.wait_ge(xn_done[ATT], GROUP_TILES * n)
                power(rstd[:, ATT, :], var_eps[:, ATT, :]).then_inc(rstd_done[ATT], 1)

            def gate_root(F):
                pool.wait_ge(gate_self, 6 * F + 3)
                power(gate_rms[:, :], gate_ms[:, :]).then_inc(gate_rms_done, 1)

            def ffn_group(layer, g):
                F = GROUPS * layer + g
                last = isinstance(g, int) and g == LAST
                if not last:
                    ln_once(F + 1)
                if layer == 0 and g >= 2:
                    inverse_lengths(pool, g - 2)
                gate_root(F)
                if layer == 0 and g >= 2:
                    unit_vectors(pool, g - 2)
                if layer == 0 and g >= 1:
                    ln_twice(g - 1)
                if layer == 0 and g >= 2:
                    low_parts(pool, g - 2)
                if not last:
                    pool.wait_ge(hi_done, F + 2 - layer)
                    low_features(pool, g + 1)

            pool.memset(ones[:, :], 1.0).then_inc(const_self, 1)
            pool.memset(neg_half[:, :], -0.5).then_inc(const_self, 1)
            pool.memset(ln_eps[:, :], LN_EPS).then_inc(const_self, 1)
            pool.wait_ge(const_self, 3)
            pool.affine_select(ident[:, :], ones[:, :], [[1, P]], ALU.is_equal, 0.0, base=0,
                               channel_multiplier=-1).then_inc(const_ready, 1)
            ln_once(0)
            for k in range(4):
                part = slice(512 * k, 512 * k + 512)
                pool.wait_ge(w2_hi_ready, k + 1)
                pool.tensor_tensor(w2_lo[:, part], w2_raw[:, part], w2_hi[:, part].bitcast(f32),
                                   ALU.subtract).then_inc(w2_ready, 1)
            ffn_group(0, 0)
            pool.wait_ge(const_ready, 1)
            pool.tensor_copy(ident16[:, :], ident[:, :]).then_inc(const_ready, 1)
            pool.memset(v_ones[:, :, :, :].rearrange("p t h r -> p (t h r)"), 0.0).then_inc(const_self, 1)
            pool.memset(q_stack[:, :, :].rearrange("p h r -> p (h r)"), 0.0).then_inc(const_self, 1)
            pool.memset(k_stack[:, :, :].rearrange("p h r -> p (h r)"), 0.0).then_inc(const_self, 1)
            pool.wait_ge(w1_ready, 4)
            pool.wait_ge(w2_ready, 4)
            pool.memset(w_raw[:, :], 0.0).then_inc(const_self, 1)
            pool.wait_ge(const_self, 7)
            pool.memset(v_ones[:, :, :, HEAD_DIM:HEAD_DIM + 1].rearrange("p t h r -> p (t h) r"), 1.0).then_inc(const_ready, 1)
            for g in range(1, GROUPS):
                ffn_group(0, g)
                if g == 1:
                    pool.memset(kT_wide[1].rearrange("p j t -> p (j t)"), 0.0).then_inc(const_ready, 1)
            for s, st in enumerate(steps):
                if not st["diagonal"]:
                    continue
                pool.wait_ge(exp_done, s + 1)
                for _, _, _, at in st["item"]:
                    region = probs[:, s % P_SLOTS, :, at:at + P]
                    pool.affine_select(region, region, [[0, 2], [1, P]], ALU.is_ge, 0.0, base=0,
                                       channel_multiplier=-1).then_inc(mask_done, 1)
                if s == 3:
                    ln_twice(LAST)
                if s == 2 * last_quad[3] + 1:
                    ln_once(GROUPS)
            ffn_groups(nc.gpsimd, 1, lambda g: ffn_group(1, g))


_INPUTS = ["L0_attn_x", "L0_attn_ln_w", "L0_attn_ln_b", "L0_attn_w_qkv", "L0_attn_w_out", "L0_ffn_gate_w", "L0_ffn_gate_b",
           "L0_ffn_rms_w", "L0_ffn_w1", "L0_ffn_b1", "L0_ffn_w2", "L0_ffn_b2"]


def kernel(**inputs):
    import concourse.bacc as bacc
    from concourse.bass_utils import run_bass_kernel_spmd

    nc = bacc.Bacc("TRN2", target_bir_lowering=False, num_devices=1)
    arrays, args = {}, []
    for name in _INPUTS:
        a = np.ascontiguousarray(inputs[name])
        arrays[f"in_{name}"] = a
        args.append(nc.dram_tensor(f"in_{name}", a.shape, mybir.dt.from_np(a.dtype), kind="ExternalInput").ap())
    out = nc.dram_tensor("out_x", (BATCH, SEQ, DIM), mybir.dt.float32, kind="ExternalOutput").ap()
    build(nc, *args, out)
    return run_bass_kernel_spmd(nc, [arrays], core_ids=[0]).results[0]["out_x"]
```
